# Optimizing a Trainium2 kernel written in Bass

```python
import numpy as np
import jax
import jax.numpy as jnp

def _softmax(x, axis=-1):
    return jax.nn.softmax(x, axis=axis)

def _gelu(x):
    return jax.nn.gelu(x, approximate=True)

def _silu(x):
    return jax.nn.silu(x)

def _sigmoid(x):
    return jax.nn.sigmoid(x)

def _layernorm(x, axis=-1, eps=1e-05):
    m = jnp.mean(x, axis=axis, keepdims=True)
    v = jnp.var(x, axis=axis, keepdims=True)
    return (x - m) / jnp.sqrt(v + eps)

def _scatter_add(tgt, idx, src, axis=0):
    return tgt.at[idx].add(src)

def _segment_sum(src, seg, n):
    return jax.ops.segment_sum(src, seg, n)
kernel_name = 'mk_adj_preln_d2_adj_r2_6da6c8'

def setup_inputs(seed: int=0):
    np.random.seed(seed)
    _w = jnp.asarray

    def _rec_inputs():
        import jax
        import jax.numpy as jnp
        _gk = jax.random.key(seed)
        x = -1.394e-06 + 0.9999 * jax.random.normal(jax.random.fold_in(_gk, 1), (64, 128, 256), jnp.float32)
        _a = jax.random.bernoulli(jax.random.fold_in(_gk, 2), 0.03125, (64, 128, 128))
        _a = jnp.logical_or(_a, jnp.swapaxes(_a, -1, -2))
        _a = jnp.logical_or(_a, jnp.eye(128, dtype=bool))
        adj = _a.astype(jnp.int32)
        return (x, adj)
    x, adj = _rec_inputs()

    def _L0_gnn_setup():
        import jax, jax.numpy as jnp
        import numpy as np
        NEG_INF = -1000000000.0
        NEG_SLOPE = 0.2

        def gat_layer(x, mask, W, a_src, a_dst, bias, concat):
            B, N, _ = x.shape
            H, F = a_src.shape
            xl = (x @ W).reshape(B, N, H, F)
            asrc = jnp.einsum('bnhf,hf->bnh', xl, a_src)
            adst = jnp.einsum('bnhf,hf->bnh', xl, a_dst)
            e = jax.nn.leaky_relu(asrc[:, :, None, :] + adst[:, None, :, :], NEG_SLOPE)
            e = jnp.where(mask[..., None], e, NEG_INF)
            attn = jax.nn.softmax(e, axis=1)
            out = jnp.einsum('bsdh,bshf->bdhf', attn, xl)
            if concat:
                out = out.reshape(B, N, H * F)
            else:
                out = out.mean(axis=2)
            return out + bias
        key = jax.random.key(seed)
        ks = jax.random.split(key, 10)
        B, N, Din, Fh, H, Dout = (8, 512, 256, 128, 4, 256)
        s = 0.05
        return {'adj': jax.random.randint(ks[0], (B, N, N), 0, 2, dtype=jnp.int32), 'x': jax.random.normal(ks[1], (B, N, Din), dtype=jnp.float32), 'W1': jax.random.normal(ks[2], (Din, H * Fh), dtype=jnp.float32) * s, 'att_src1': jax.random.normal(ks[3], (H, Fh), dtype=jnp.float32) * s, 'att_dst1': jax.random.normal(ks[4], (H, Fh), dtype=jnp.float32) * s, 'b1': jax.random.normal(ks[5], (H * Fh,), dtype=jnp.float32) * s, 'W2': jax.random.normal(ks[6], (H * Fh, Dout), dtype=jnp.float32) * s, 'att_src2': jax.random.normal(ks[7], (1, Dout), dtype=jnp.float32) * s, 'att_dst2': jax.random.normal(ks[8], (1, Dout), dtype=jnp.float32) * s, 'b2': jax.random.normal(ks[9], (Dout,), dtype=jnp.float32) * s}
    _L0_gnn_all = _L0_gnn_setup()
    _L0_gnn_in = {k: v for k, v in _L0_gnn_all.items() if k in ('W1', 'att_src1', 'att_dst1', 'b1', 'W2', 'att_src2', 'att_dst2', 'b2')}
    del _L0_gnn_all

    def _L1_gnn_setup():
        import jax, jax.numpy as jnp
        import numpy as np
        B, N, D = (8, 512, 256)
        NH = 8
        DK = D // NH
        key = jax.random.key(seed)
        ks = jax.random.split(key, 6)
        x = jax.random.normal(ks[0], (B, N, D), dtype=jnp.float32)
        adj = jax.random.randint(ks[1], (B, N, N), 0, 2, dtype=jnp.int32)
        adj = jnp.maximum(adj, jnp.eye(N, dtype=jnp.int32)[None])
        s = 1.0 / np.sqrt(D)
        Wq = jax.random.normal(ks[2], (D, D), dtype=jnp.float32) * s
        Wk = jax.random.normal(ks[3], (D, D), dtype=jnp.float32) * s
        Wv = jax.random.normal(ks[4], (D, D), dtype=jnp.float32) * s
        Wo = jax.random.normal(ks[5], (D, D), dtype=jnp.float32) * s
        return {'x': x, 'adj': adj, 'Wq': Wq, 'Wk': Wk, 'Wv': Wv, 'Wo': Wo}
    _L1_gnn_all = _L1_gnn_setup()
    _L1_gnn_in = {k: v for k, v in _L1_gnn_all.items() if k in ('Wq', 'Wk', 'Wv', 'Wo')}
    del _L1_gnn_all
    return {'x': x, 'adj': adj, 'L0_gnn_W1': _L0_gnn_in['W1'], 'L0_gnn_att_src1': _L0_gnn_in['att_src1'], 'L0_gnn_att_dst1': _L0_gnn_in['att_dst1'], 'L0_gnn_b1': _L0_gnn_in['b1'], 'L0_gnn_W2': _L0_gnn_in['W2'], 'L0_gnn_att_src2': _L0_gnn_in['att_src2'], 'L0_gnn_att_dst2': _L0_gnn_in['att_dst2'], 'L0_gnn_b2': _L0_gnn_in['b2'], 'L1_gnn_Wq': _L1_gnn_in['Wq'], 'L1_gnn_Wk': _L1_gnn_in['Wk'], 'L1_gnn_Wv': _L1_gnn_in['Wv'], 'L1_gnn_Wo': _L1_gnn_in['Wo']}

def reference(x, adj, L0_gnn_W1, L0_gnn_att_src1, L0_gnn_att_dst1, L0_gnn_b1, L0_gnn_W2, L0_gnn_att_src2, L0_gnn_att_dst2, L0_gnn_b2, L1_gnn_Wq, L1_gnn_Wk, L1_gnn_Wv, L1_gnn_Wo):
    import jax
    import jax.numpy as jnp

    def _L0_gnn_ref(adj, x, W1, att_src1, att_dst1, b1, W2, att_src2, att_dst2, b2):
        import jax, jax.numpy as jnp
        import numpy as np
        NEG_INF = -1000000000.0
        NEG_SLOPE = 0.2

        def gat_layer(x, mask, W, a_src, a_dst, bias, concat):
            B, N, _ = x.shape
            H, F = a_src.shape
            xl = (x @ W).reshape(B, N, H, F)
            asrc = jnp.einsum('bnhf,hf->bnh', xl, a_src)
            adst = jnp.einsum('bnhf,hf->bnh', xl, a_dst)
            e = jax.nn.leaky_relu(asrc[:, :, None, :] + adst[:, None, :, :], NEG_SLOPE)
            e = jnp.where(mask[..., None], e, NEG_INF)
            attn = jax.nn.softmax(e, axis=1)
            out = jnp.einsum('bsdh,bshf->bdhf', attn, xl)
            if concat:
                out = out.reshape(B, N, H * F)
            else:
                out = out.mean(axis=2)
            return out + bias
        B, N, _ = adj.shape
        mask = (adj > 0) | jnp.eye(N, dtype=bool)[None]
        h = jax.nn.elu(gat_layer(x, mask, W1, att_src1, att_dst1, b1, concat=True))
        h = gat_layer(h, mask, W2, att_src2, att_dst2, b2, concat=False)
        return h

    def _L1_gnn_ref(x, adj, Wq, Wk, Wv, Wo):
        import jax, jax.numpy as jnp
        import numpy as np
        B, N, D = (8, 512, 256)
        NH = 8
        DK = D // NH
        b, n, d = x.shape
        sqrt_dk = jnp.asarray(np.sqrt(DK), dtype=x.dtype)

        def heads(t):
            return t.reshape(b, n, NH, DK).transpose(0, 2, 1, 3)
        q = heads(x @ Wq)
        k = heads(x @ Wk)
        v = heads(x @ Wv)
        scores = jnp.einsum('bhnd,bhmd->bhnm', q, k) / sqrt_dk
        mask = adj.astype(bool)[:, None]
        scores = jnp.where(mask, scores, -jnp.inf)
        attn = jax.nn.softmax(scores, axis=-1)
        out = jnp.einsum('bhnm,bhmd->bhnd', attn, v)
        out = out.transpose(0, 2, 1, 3).reshape(b, n, d)
        return jax.nn.relu(out) @ Wo
    h = jnp.maximum(_layernorm(x, axis=-1), 0.0)
    x = x + _L0_gnn_ref(adj, h, L0_gnn_W1, L0_gnn_att_src1, L0_gnn_att_dst1, L0_gnn_b1, L0_gnn_W2, L0_gnn_att_src2, L0_gnn_att_dst2, L0_gnn_b2)
    h = jnp.maximum(_layernorm(x, axis=-1), 0.0)
    x = x + _L1_gnn_ref(h, adj, L1_gnn_Wq, L1_gnn_Wk, L1_gnn_Wv, L1_gnn_Wo)
    return x

_drawn_inputs = setup_inputs


def setup_inputs(seed=0):
    import zlib

    import numpy as np

    out = dict(_drawn_inputs(seed))
    spreads = {}
    factors = {'L0_gnn_att_src1': 4.036,
     'L0_gnn_att_dst1': 8.0,
     'L0_gnn_att_src2': 8.0,
     'L0_gnn_att_dst2': 30.139}
    for name, (base, spread) in spreads.items():
        noise = np.random.default_rng([zlib.crc32(name.encode()), seed]).standard_normal(out[name].shape)
        drawn = base * np.exp(spread * noise) if base else spread * noise
        out[name] = jnp.asarray(drawn.astype(out[name].dtype))
    for name, factor in factors.items():
        out[name] = (out[name] * factor).astype(out[name].dtype)
    return out
```

```python
from contextlib import ExitStack

import concourse.bass as bass
from concourse import mybir

F32 = mybir.dt.float32
BF16 = mybir.dt.bfloat16
I32 = mybir.dt.int32
ALU = mybir.AluOpType
ACT = mybir.ActivationFunctionType
AX = mybir.AxisListType

EPS = 1e-5
SLOPE = 0.2
BIG = 1e30
UNROLL = 4
P_, A_, B_, C_, D_ = range(5)


class Graph:

    def __init__(self, base, unrolled, lag, count):
        self.n = base + (unrolled - lag)
        self.four = (unrolled - lag) % 4
        self.two = (unrolled - lag) % 2
        self.dma = base * 4 + 16 * ((unrolled - lag) // 4 + 1)
        self.active = not isinstance(base, int) or 0 <= self.n < count


def wait(eng, sem, value):
    if not isinstance(value, int) or value > 0:
        eng.wait_ge(sem, value)


def done(eng, sem, g):
    wait(eng, sem, g.n + 1)


def free(eng, sem, g, ring=2):
    wait(eng, sem, g.n + 1 - ring)


def gnn_kernel(nc, x, adj, W1, att_src1, att_dst1, b1, W2, att_src2, att_dst2, b2, Wq, Wk, Wv, Wo, out):
    G, N, D = x.shape
    H, F = att_src1.shape
    HF = H * F
    KD = D // 128
    NH, DK = 8, D // 8
    HALF = HF // 2 + 2 * (H // 2)
    SCALE = float(DK) ** -0.5

    ctx = ExitStack()
    with ctx:
        def sb(name, shape, dt=F32):
            return ctx.enter_context(nc.sbuf_tensor(name, shape, dt))

        def sem(name):
            return ctx.enter_context(nc.semaphore(name))

        ident = sb("ident", [128, 128])
        ident_bf = sb("ident_bf", [128, 128], BF16)
        offdiag = sb("offdiag", [128, 128])
        ones = sb("ones", [128, 128])
        minus_half = sb("minus_half", [128, 1])
        pause = sb("pause", [128, 1])
        w1 = sb("w1", [128, KD, 2, HALF])
        w2 = sb("w2", [128, H, D + 2])
        wqk = sb("wqk", [128, KD, 2, D])
        wv = sb("wv", [128, KD, D])
        wo = sb("wo", [128, KD, D])
        b1_all = sb("b1_all", [128, HF])
        b2_all = sb("b2_all", [128, D])
        att1 = sb("att1", [128, 2, HF])
        att2 = sb("att2", [128, 2, D])
        prod = sb("prod", [128, 4, HF])

        x_in = sb("x_in", [128, 4, D])
        adj_in = sb("adj_in", [128, 4, N], I32)
        mask_gat = sb("mask_gat", [128, 4, N], BF16)
        mask_mha = sb("mask_mha", [128, 4, N], BF16)
        stats = sb("stats", [128, 2, 2, 6])
        mv = sb("mv", [128, 2, 2, 2])
        var = sb("var", [128, 2, 2])
        rstd = sb("rstd", [128, 2, 2])
        z = sb("z", [128, 2, 2, D])
        hT = sb("hT", [128, 2, D])
        xl = sb("xl", [128, 2, HF])
        ab = sb("ab", [128, 2, 2, 4])
        diag = sb("diag", [128, 2, HF])
        zb = sb("zb", [128, 2, HF])
        lr = sb("lr", [128, 2, HF])
        mx = sb("mx", [128, 2, H])
        nmx = sb("nmx", [128, 2, H])
        eT = sb("eT", [128, 2, HF])
        sm = sb("sm", [128, 2, H])
        rs = sb("rs", [128, 2, H])
        eTn = sb("eTn", [128, 2, HF])
        en = sb("en", [128, 2, HF])
        ex = sb("ex", [128, 2, HF])
        ex1 = sb("ex1", [128, 2, HF])
        h1T = sb("h1T", [128, 2, HF])
        xl2 = sb("xl2", [128, 2, D])
        ab2 = sb("ab2", [128, 2, 2])
        diag2 = sb("diag2", [128, 2, N])
        zb2 = sb("zb2", [128, 2, N])
        lr2 = sb("lr2", [128, 2, N])
        mx2 = sb("mx2", [128, 2, 1])
        nmx2 = sb("nmx2", [128, 2, 1])
        eT2 = sb("eT2", [128, 2, N])
        sm2 = sb("sm2", [128, 2, 1])
        rs2 = sb("rs2", [128, 2, 1])
        en2 = sb("en2", [128, 2, N])
        x1 = sb("x1", [128, 4, D])
        h2T = sb("h2T", [128, 2, D])
        qkT = sb("qkT", [128, 2, 4, N])
        vv = sb("vv", [128, 2, NH, DK + 1])
        mx3 = sb("mx3", [128, 2, NH])
        nmx3 = sb("nmx3", [128, 2, NH])
        e3 = sb("e3", [128, 2, NH, N])
        e3T = sb("e3T", [128, 2, NH, N])
        rs3 = sb("rs3", [128, 2, NH])
        att = sb("att", [128, 2, D])
        attT = sb("attT", [128, 2, D])
        x_out = sb("x_out", [128, 4, D])

        bank = ctx.enter_context(nc.psum_tensor("bank", [128, 8, 512], F32))
        XL, EM, X2, AV, Z2, Z = bank[:, 0:2, :], bank[:, 2:4, :], bank[:, 4], bank[:, 5], bank[:, 6], bank[:, 7]
        QK, ET2, T3, V, O2, S = bank[:, 0], bank[:, 4], bank[:, 5], bank[:, 1], bank[:, 6], bank[:, 2:4, :]
        T2, ET, WO, T1, O1 = bank[:, 4], bank[:, 7], bank[:, 5], bank[:, 0], bank[:, 6]

        names = """ident_set ones_set const_set weights_in att_in w1_prod w1_set w2_prod w2_set
            masks_set stats_set mv_set var_set rstd_set z_set
            stats2_set mv2_set var2_set rstd2_set z2_set
            t1_done hT_set xl_done xl_set ab_set diag_set zsc_done zb_set lr_set mx_set nmx_set eT_set rs_set eTn_set
            et_done en_set o1_done ex_set ex1_set h1T_set x2_done xl2_set ab2_set diag2_set zsc2_done zb2_set lr2_set
            mx2_set nmx2_set eT2_set rs2_set et2_done en2_set o2_done x1_set t2_done h2T_set qk_done qkT_set v_done
            vv_set s_half s_done mx3_set nmx3_set e3_set em_done e3T_set av_done rs3_set att_set t3_done attT_set wo_done
            x_out_set""".split()
        s = {n: sem(n) for n in names}
        x_here = [sem(f"x_here{i}") for i in range(4)]
        adj_here = [sem(f"adj_here{i}") for i in range(4)]
        stored = [sem(f"stored{i}") for i in range(4)]

        def head_at(j):
            return j // 4 + (0, 4, 2, 6)[j % 4]

        def steps(eng, body):
            last = G + D_
            for t in range(2 * UNROLL):
                body([Graph(t - t % UNROLL, t % UNROLL, lag, G) for lag in range(5)])
            with eng.Fori(2 * UNROLL, G - UNROLL + 1, UNROLL) as t:
                for u in range(UNROLL):
                    body([Graph(t, u, lag, G) for lag in range(5)])
            for t in range(G, last):
                body([Graph(t - t % UNROLL, t % UNROLL, lag, G) for lag in range(5)])

        def run(body_functions, graphs):
            for function, phase in body_functions:
                if graphs[phase].active:
                    function(graphs[phase])

        block = ctx.enter_context(nc.Block())

        @block.sync
        def _(sp):
            for k in range(KD):
                sp.dma_start(w1[:, k, :, 0:HF // 2], W1[k * 128:(k + 1) * 128, :].rearrange("p (a c) -> p a c", a=2)).then_inc(s["weights_in"], 16)
            for k in range(2):
                sp.dma_start(att1[:, k, :], (att_src1, att_dst1)[k].rearrange("h f -> (h f)").partition_broadcast(128)).then_inc(s["att_in"], 16)
                sp.dma_start(att2[:, k, :], (att_src2, att_dst2)[k].rearrange("h f -> (h f)").partition_broadcast(128)).then_inc(s["att_in"], 16)
            sp.dma_start(b1_all[:, :], b1.partition_broadcast(128)).then_inc(s["weights_in"], 16)
            sp.dma_start(b2_all[:, :], b2.partition_broadcast(128)).then_inc(s["weights_in"], 16)
            sp.dma_start(w2[:, :, 0:D], W2.rearrange("(k p) n -> p k n", p=128)).then_inc(s["weights_in"], 16)
            sp.dma_start(wqk[:, :, 0, :], Wq.rearrange("(k p) n -> p k n", p=128)).then_inc(s["weights_in"], 16)
            sp.dma_start(wqk[:, :, 1, :], Wk.rearrange("(k p) n -> p k n", p=128)).then_inc(s["weights_in"], 16)
            sp.dma_start(wv[:, :, :], Wv.rearrange("(k p) n -> p k n", p=128)).then_inc(s["weights_in"], 16)
            sp.dma_start(wo[:, :, :], Wo.rearrange("(k p) n -> p k n", p=128)).then_inc(s["weights_in"], 16)

            def load(g):
                free(sp, s["x1_set"], g, 4)
                sp.dma_start(x_in[:, g.four, :], x[bass.ds(g.n, 1)].rearrange("a n d -> (a n) d")).then_inc(x_here[g.four], 16)
                free(sp, s["masks_set"], g, 4)
                sp.dma_start(adj_in[:, g.four, :], adj[bass.ds(g.n, 1)].rearrange("a n d -> (a n) d")).then_inc(adj_here[g.four], 16)

            def store(g):
                done(sp, s["x_out_set"], g)
                sp.dma_start(out[bass.ds(g.n, 1)].rearrange("a n d -> (a n) d"), x_out[:, g.four, :]).then_inc(stored[g.four], 16)

            steps(sp, lambda graphs: run([(load, P_), (store, D_)], graphs))
            for n in range(4):
                sp.wait_ge(stored[n], 16 * (G // 4))

        @block.gpsimd
        def _(pool):
            pool.memset(ident[:, :], 0.0).then_inc(s["ident_set"], 1)
            pool.memset(offdiag[:, :], -BIG).then_inc(s["ident_set"], 1)
            pool.memset(ones[:, :], 1.0).then_inc(s["ones_set"], 1)
            pool.memset(minus_half[:, :], -0.5).then_inc(s["ones_set"], 1)
            pool.memset(vv[:, :, :, DK:DK + 1], 1.0).then_inc(s["ones_set"], 1)
            pool.wait_ge(s["ident_set"], 2)
            for tile, fill in ((ident, 1.0), (offdiag, 0.0)):
                pool.affine_select(out=tile[:, :], in_=tile[:, :], compare_op=ALU.not_equal, fill=fill, base=0,
                                   pattern=[[-1, 128]], channel_multiplier=1).then_inc(s["ident_set"], 1)
            pool.wait_ge(s["ident_set"], 4)
            pool.tensor_copy(ident_bf[:, :], ident[:, :]).then_inc(s["ident_set"], 1)

            def diagonals(g):
                done(pool, s["ab_set"], g)
                free(pool, s["zsc_done"], g)
                pool.tensor_tensor(
                    diag[:, g.two, :].rearrange("p (a h n) -> p a h n", a=2, h=2),
                    ident[:, :].unsqueeze(1).unsqueeze(1).to_broadcast((128, 2, 2, N)),
                    ab[:, g.two, :, 0:2].unsqueeze(3).to_broadcast((128, 2, 2, N)), ALU.mult).then_inc(s["diag_set"], 1)

            def rsqrt(g, which, var_set, free_sem, rstd_set):
                done(pool, s[var_set], g)
                free(pool, s[free_sem], g)
                pool.tensor_tensor(rstd[:, g.two, which:which + 1], var[:, g.two, which:which + 1], minus_half[:, :], ALU.pow).then_inc(s[rstd_set], 1)

            def rsqrt1(g):
                rsqrt(g, 0, "var_set", "z_set", "rstd_set")

            def rsqrt2(g):
                rsqrt(g, 1, "var2_set", "z2_set", "rstd2_set")

            steps(pool, lambda graphs: run([(rsqrt1, P_), (diagonals, A_), (rsqrt2, B_)], graphs))

        @block.scalar
        def _(act):
            def relu1(g):
                done(act, s["t1_done"], g)
                free(act, s["xl_done"], g)
                act.activation(hT[:, g.two, :], T1[:, 0:D], ACT.Relu).then_inc(s["hT_set"], 1)

            def gat1_exp(g):
                done(act, s["nmx_set"], g)
                free(act, s["eTn_set"], g)
                for h in range(H):
                    ins = act.activation(eT[:, g.two, h * N:(h + 1) * N], lr[:, g.two, h * N:(h + 1) * N], ACT.Exp,
                                         bias=nmx[:, g.two, h:h + 1], accum_out=sm[:, g.two, h:h + 1])
                ins.then_inc(s["eT_set"], 1)

            def gat1_copy(g):
                done(act, s["et_done"], g)
                free(act, s["o1_done"], g)
                act.activation(en[:, g.two, :], ET[:, :], ACT.Copy).then_inc(s["en_set"], 1)

            def elu_exp(g):
                done(act, s["o1_done"], g)
                free(act, s["ex1_set"], g)
                act.activation(ex[:, g.two, :], O1[:, :], ACT.Exp).then_inc(s["ex_set"], 1)

            def gat2_exp(g):
                done(act, s["nmx2_set"], g)
                free(act, s["et2_done"], g)
                free(act, s["rs2_set"], g)
                act.activation(eT2[:, g.two, :], lr2[:, g.two, :], ACT.Exp, bias=nmx2[:, g.two, :],
                               accum_out=sm2[:, g.two, :]).then_inc(s["eT2_set"], 1)

            def gat2_copy(g):
                done(act, s["et2_done"], g)
                free(act, s["o2_done"], g)
                act.activation(en2[:, g.two, :], ET2[:, 0:N], ACT.Copy).then_inc(s["en2_set"], 1)

            def relu2(g):
                done(act, s["t2_done"], g)
                free(act, s["v_done"], g)
                act.activation(h2T[:, g.two, :], T2[:, 0:D], ACT.Relu).then_inc(s["h2T_set"], 1)

            def qk_copy(g):
                done(act, s["qk_done"], g)
                free(act, s["s_done"], g)
                act.activation(qkT[:, g.two, :, :], QK.rearrange("p (c n) -> p c n", c=4), ACT.Copy).then_inc(s["qkT_set"], 1)

            def mha_exp(g):
                done(act, s["nmx3_set"], g)
                free(act, s["em_done"], g)
                for h in range(NH):
                    ins = act.activation(e3[:, g.two, h, :], S[:, h // 4, (h % 4) * N:(h % 4 + 1) * N], ACT.Exp,
                                         bias=nmx3[:, g.two, h:h + 1], scale=SCALE)
                ins.then_inc(s["e3_set"], 1)

            def mha_copy(g):
                done(act, s["em_done"], g)
                free(act, s["av_done"], g)
                act.activation(e3T[:, g.two, :, :], EM.rearrange("p b (h n) -> p (b h) n", h=4), ACT.Copy).then_inc(s["e3T_set"], 1)

            def att_copy(g):
                done(act, s["t3_done"], g)
                free(act, s["wo_done"], g)
                act.activation(attT[:, g.two, :], T3[:, 0:D], ACT.Copy).then_inc(s["attT_set"], 1)

            steps(act, lambda graphs: run([
                (elu_exp, B_), (mha_copy, D_), (gat2_exp, B_), (qk_copy, C_), (gat2_copy, B_),
                (att_copy, D_), (gat1_exp, A_), (relu2, B_), (gat1_copy, A_), (relu1, P_), (mha_exp, C_),
            ], graphs))

        @block.vector
        def _(dve):
            dve.wait_ge(s["weights_in"], 16 * 9)
            dve.wait_ge(s["att_in"], 16 * 4)
            for k in range(KD):
                for j in range(2):
                    dve.tensor_tensor(prod[:, 2 * k + j, :].rearrange("p (a c) -> p a c", a=2), w1[:, k, :, 0:HF // 2],
                                      att1[:, j, :].rearrange("p (a c) -> p a c", a=2), ALU.mult).then_inc(s["w1_prod"], 1)
            dve.wait_ge(s["w1_prod"], 2 * KD)
            for k in range(KD):
                for j in range(2):
                    dve.tensor_reduce(w1[:, k, :, HF // 2 + 2 * j:HF // 2 + 2 * j + 2],
                                      prod[:, 2 * k + j, :].rearrange("p (a h f) -> p a h f", a=2, h=2), AX.X, ALU.add).then_inc(s["w1_set"], 1)
            dve.wait_ge(s["w1_set"], 2 * KD)
            for j in range(2):
                for half in range(2):
                    dve.tensor_tensor(prod[:, 2 * j + half, :].rearrange("p (a c) -> p a c", a=2), w2[:, 2 * half:2 * half + 2, 0:D],
                                      att2[:, j, :].unsqueeze(1).to_broadcast((128, 2, D)), ALU.mult).then_inc(s["w2_prod"], 1)
            dve.wait_ge(s["w2_prod"], 4)
            for j in range(2):
                dve.tensor_reduce(w2[:, :, D + j:D + j + 1], prod[:, 2 * j:2 * j + 2, :].rearrange("p b (a c) -> p b a c", a=2),
                                  AX.X, ALU.add).then_inc(s["w2_set"], 1)

            def moments(g, which, src, stats_set, mv_set, var_set):
                dve.bn_stats(stats[:, g.two, which, :], src).then_inc(s[stats_set], 1)
                done(dve, s[stats_set], g)
                dve.memset(pause[:, :], 0.0)
                dve.bn_aggr(mv[:, g.two, which, :], stats[:, g.two, which, :]).then_inc(s[mv_set], 1)
                done(dve, s[mv_set], g)
                dve.tensor_scalar(var[:, g.two, which:which + 1], mv[:, g.two, which, 1:2], EPS, None, ALU.add).then_inc(s[var_set], 1)

            def normed(g, which, src, rstd_set, free_sem, z_set):
                done(dve, s[rstd_set], g)
                free(dve, s[free_sem], g)
                dve.tensor_scalar(z[:, g.two, which, :], src, mv[:, g.two, which, 0:1], rstd[:, g.two, which:which + 1],
                                  ALU.subtract, ALU.mult).then_inc(s[z_set], 1)

            def masks(g):
                dve.wait_ge(adj_here[g.four], g.dma)
                free(dve, s["s_done"], g, 4)
                dve.tensor_scalar(mask_mha[:, g.four, :], adj_in[:, g.four, :], 0.0, -BIG, ALU.is_equal, ALU.mult)
                dve.scalar_tensor_tensor(out=mask_gat[:, g.four, :], in0=adj_in[:, g.four, :], scalar=0.0, in1=offdiag[:, :],
                                         op0=ALU.is_le, op1=ALU.mult).then_inc(s["masks_set"], 1)

            def norm1_moments(g):
                dve.wait_ge(x_here[g.four], g.dma)
                moments(g, 0, x_in[:, g.four, :], "stats_set", "mv_set", "var_set")

            def norm1_apply(g):
                normed(g, 0, x_in[:, g.four, :], "rstd_set", "t1_done", "z_set")

            def elu(g):
                done(dve, s["ex_set"], g)
                dve.tensor_scalar(ex1[:, g.two, :], ex[:, g.two, :], 1.0, 1.0, ALU.min, ALU.subtract).then_inc(s["ex1_set"], 1)
                done(dve, s["ex1_set"], g)
                free(dve, s["x2_done"], g)
                dve.tensor_tensor(h1T[:, g.two, :], O1[:, :], ex1[:, g.two, :], ALU.max).then_inc(s["h1T_set"], 1)

            def xl_evac(g):
                done(dve, s["xl_done"], g)
                free(dve, s["diag_set"], g)
                dve.tensor_copy(ab[:, g.two, :, :], XL[:, :, HF // 2:HALF]).then_inc(s["ab_set"], 1)
                free(dve, s["o1_done"], g)
                dve.tensor_tensor(xl[:, g.two, :].rearrange("p (a c) -> p a c", a=2), XL[:, :, 0:HF // 2],
                                  b1_all[:, :].rearrange("p (a c) -> p a c", a=2), ALU.add).then_inc(s["xl_set"], 1)

            def xl2_evac(g):
                done(dve, s["x2_done"], g)
                dve.tensor_copy(ab2[:, g.two, :], X2[:, D:D + 2]).then_inc(s["ab2_set"], 1)
                free(dve, s["o2_done"], g)
                dve.tensor_tensor(xl2[:, g.two, :], X2[:, 0:D], b2_all[:, :], ALU.add).then_inc(s["xl2_set"], 1)
                done(dve, s["ab2_set"], g)
                free(dve, s["zsc2_done"], g)
                dve.tensor_scalar(diag2[:, g.two, :], ident[:, :], ab2[:, g.two, 0:1], None, ALU.mult).then_inc(s["diag2_set"], 1)

            def att_norm(g):
                done(dve, s["av_done"], g)
                av = AV[:, 0:NH * (DK + 1)].rearrange("p (h c) -> p h c", h=NH)
                dve.reciprocal(rs3[:, g.two, :].unsqueeze(2), av[:, :, DK:DK + 1]).then_inc(s["rs3_set"], 1)
                done(dve, s["rs3_set"], g)
                free(dve, s["t3_done"], g)
                dve.scalar_tensor_tensor(out=att[:, g.two, :].rearrange("p (h c) -> p h c", h=NH), in0=av[:, :, 0:DK], scalar=0.0,
                                         in1=rs3[:, g.two, :].unsqueeze(2).to_broadcast((128, NH, DK)),
                                         op0=ALU.max, op1=ALU.mult).then_inc(s["att_set"], 1)

            def gat2_scores(g):
                done(dve, s["zsc2_done"], g)
                dve.tensor_scalar(zb2[:, g.two, :], Z2[:, 0:N], ab2[:, g.two, 1:2], None, ALU.add).then_inc(s["zb2_set"], 1)
                done(dve, s["zb2_set"], g)
                free(dve, s["eT2_set"], g)
                dve.scalar_tensor_tensor(out=lr2[:, g.two, :], in0=zb2[:, g.two, :], scalar=SLOPE, in1=zb2[:, g.two, :],
                                         op0=ALU.mult, op1=ALU.max).then_inc(s["lr2_set"], 1)
                done(dve, s["lr2_set"], g)
                dve.tensor_reduce(mx2[:, g.two, :], lr2[:, g.two, :], AX.X, ALU.max).then_inc(s["mx2_set"], 1)
                done(dve, s["mx2_set"], g)
                dve.tensor_scalar(nmx2[:, g.two, :], mx2[:, g.two, :], -1.0, None, ALU.mult).then_inc(s["nmx2_set"], 1)

            def gat1_scores(g):
                done(dve, s["zsc_done"], g)
                dve.tensor_tensor(zb[:, g.two, :].rearrange("p (a h n) -> p a h n", a=2, h=2),
                                  Z.rearrange("p (a h n) -> p a h n", a=2, h=2),
                                  ab[:, g.two, :, 2:4].unsqueeze(3).to_broadcast((128, 2, 2, N)), ALU.add).then_inc(s["zb_set"], 1)
                done(dve, s["zb_set"], g)
                free(dve, s["eT_set"], g)
                dve.scalar_tensor_tensor(out=lr[:, g.two, :], in0=zb[:, g.two, :], scalar=SLOPE, in1=zb[:, g.two, :],
                                         op0=ALU.mult, op1=ALU.max).then_inc(s["lr_set"], 1)
                done(dve, s["lr_set"], g)
                dve.tensor_reduce(mx[:, g.two, :], lr[:, g.two, :].rearrange("p (h n) -> p h n", h=H), AX.X, ALU.max).then_inc(s["mx_set"], 1)
                done(dve, s["mx_set"], g)
                dve.tensor_scalar(nmx[:, g.two, :], mx[:, g.two, :], -1.0, None, ALU.mult).then_inc(s["nmx_set"], 1)

            def gat2_recip(g):
                done(dve, s["eT2_set"], g)
                dve.reciprocal(rs2[:, g.two, :], sm2[:, g.two, :]).then_inc(s["rs2_set"], 1)

            def v_evac(g):
                done(dve, s["v_done"], g)
                free(dve, s["av_done"], g)
                dve.tensor_copy(vv[:, g.two, :, 0:DK], V[:, 0:D].rearrange("p (h c) -> p h c", h=NH)).then_inc(s["vv_set"], 1)

            def residual1(g):
                done(dve, s["o2_done"], g)
                done(dve, s["rs2_set"], g)
                dve.scalar_tensor_tensor(out=x1[:, g.four, :], in0=O2[:, 0:D], scalar=rs2[:, g.two, :], in1=x_in[:, g.four, :],
                                         op0=ALU.mult, op1=ALU.add).then_inc(s["x1_set"], 1)

            def norm2_moments(g):
                done(dve, s["x1_set"], g)
                moments(g, 1, x1[:, g.four, :], "stats2_set", "mv2_set", "var2_set")

            def norm2_apply(g):
                normed(g, 1, x1[:, g.four, :], "rstd2_set", "t2_done", "z2_set")

            def gat1_normalise(g):
                done(dve, s["eT_set"], g)
                dve.reciprocal(rs[:, g.two, :], sm[:, g.two, :]).then_inc(s["rs_set"], 1)
                done(dve, s["rs_set"], g)
                free(dve, s["et_done"], g)
                for h in range(H):
                    ins = dve.tensor_scalar(eTn[:, g.two, h * N:(h + 1) * N], eT[:, g.two, h * N:(h + 1) * N], rs[:, g.two, h:h + 1], None, ALU.mult)
                ins.then_inc(s["eTn_set"], 1)

            def mha_max(g):
                done(dve, s["s_done"], g)
                dve.tensor_reduce(mx3[:, g.two, :], S.rearrange("p b (h n) -> p (b h) n", h=4), AX.X, ALU.max).then_inc(s["mx3_set"], 1)
                done(dve, s["mx3_set"], g)
                free(dve, s["e3_set"], g)
                dve.tensor_scalar(nmx3[:, g.two, :], mx3[:, g.two, :], -SCALE, None, ALU.mult).then_inc(s["nmx3_set"], 1)

            def residual2(g):
                done(dve, s["wo_done"], g)
                if not isinstance(g.n, int) or g.n >= 4:
                    dve.wait_ge(stored[g.four], g.dma - 16)
                dve.tensor_tensor(x_out[:, g.four, :], WO[:, 0:D], x1[:, g.four, :], ALU.add).then_inc(s["x_out_set"], 1)

            dve.wait_ge(s["ident_set"], 5)
            steps(dve, lambda graphs: run([
                (elu, B_), (norm1_moments, P_), (masks, P_), (xl_evac, A_), (xl2_evac, B_), (norm1_apply, P_), (att_norm, D_), (gat2_scores, B_),
                (gat1_scores, A_), (gat2_recip, B_), (v_evac, C_), (residual1, B_), (norm2_moments, B_), (gat1_normalise, A_),
                (norm2_apply, B_), (mha_max, C_), (residual2, D_),
            ], graphs))

        @block.tensor
        def _(pe):
            pe.wait_ge(s["weights_in"], 16 * 9)
            pe.wait_ge(s["ident_set"], 5)
            pe.wait_ge(s["ones_set"], 3)
            pe.wait_ge(s["w1_set"], 2 * KD)
            pe.wait_ge(s["w2_set"], 2)

            def chunks(tile, g):
                return tile[:, g.two, :].rearrange("p (k n) -> p k n", n=128)

            def project1(g):
                done(pe, s["hT_set"], g)
                free(pe, s["vv_set"], g, 3)
                for a in range(2):
                    for k in range(KD):
                        ins = pe.matmul(XL[:, a, 0:HALF], chunks(hT, g)[:, k], w1[:, k, a, :], start=k == 0, stop=k == KD - 1)
                ins.then_inc(s["xl_done"], 1)

            def mha_transpose(g):
                done(pe, s["e3_set"], g)
                for h in range(NH):
                    ins = pe.transpose(EM[:, h // 4, (h % 4) * N:(h % 4 + 1) * N], e3[:, g.two, h, :], ident[:, :])
                ins.then_inc(s["em_done"], 1)

            def project2(g):
                done(pe, s["h1T_set"], g)
                free(pe, s["h2T_set"], g, 1)
                for k in range(H):
                    ins = pe.matmul(X2[:, 0:D + 2], h1T[:, g.two, k * F:(k + 1) * F], w2[:, k, :], start=k == 0, stop=k == H - 1)
                ins.then_inc(s["x2_done"], 1)

            def mha_av(g):
                done(pe, s["e3T_set"], g)
                done(pe, s["vv_set"], g)
                free(pe, s["x_out_set"], g, 1)
                for j in range(NH):
                    h = head_at(j)
                    ins = pe.matmul(AV[:, h * (DK + 1):(h + 1) * (DK + 1)], e3T[:, g.two, j, :], vv[:, g.two, h, :], start=True, stop=True)
                ins.then_inc(s["av_done"], 1)

            def scores2(g):
                done(pe, s["diag2_set"], g)
                done(pe, s["h1T_set"], g)
                pe.matmul(Z2[:, 0:N], ones[:, :], diag2[:, g.two, :], start=True, stop=False)
                pe.matmul(Z2[:, 0:N], mask_gat[:, g.four, :], ident_bf[:, :], start=False, stop=True).then_inc(s["zsc2_done"], 1)

            def scores1(g):
                done(pe, s["diag_set"], g)
                done(pe, s["masks_set"], g)
                free(pe, s["en_set"], g, 1)
                pe.matmul(Z[:, :], ones[:, :], diag[:, g.two, :], start=True, stop=False)
                pe.matmul(Z[:, :], mask_gat[:, g.four, :], ident_bf[:, :].unsqueeze(1).to_broadcast((128, H, N)),
                          start=False, stop=True).then_inc(s["zsc_done"], 1)

            def qk(g):
                done(pe, s["h2T_set"], g)
                wait(pe, s["xl_set"], min(g.n + 3, G) if isinstance(g.n, int) else g.n + 3)
                for c in range(4):
                    for k in range(KD):
                        ins = pe.matmul(QK[:, c * N:(c + 1) * N], wqk[:, k, c // 2, (c % 2) * 128:(c % 2 + 1) * 128], chunks(h2T, g)[:, k],
                                        start=k == 0, stop=k == KD - 1)
                ins.then_inc(s["qk_done"], 1)

            def transpose2(g):
                done(pe, s["eT2_set"], g)
                done(pe, s["xl2_set"], g)
                pe.transpose(ET2[:, 0:N], eT2[:, g.two, :], ident[:, :]).then_inc(s["et2_done"], 1)

            def att_transpose(g):
                done(pe, s["att_set"], g)
                for k in range(KD):
                    ins = pe.transpose(T3[:, k * N:(k + 1) * N], att[:, g.two, k * 128:(k + 1) * 128], ident[:, :])
                ins.then_inc(s["t3_done"], 1)

            def project_v(g):
                for k in range(KD):
                    ins = pe.matmul(V[:, 0:D], chunks(h2T, g)[:, k], wv[:, k, :], start=k == 0, stop=k == KD - 1)
                ins.then_inc(s["v_done"], 1)

            def aggregate2(g):
                done(pe, s["en2_set"], g)
                pe.matmul(O2[:, 0:D], en2[:, g.two, :], xl2[:, g.two, :], start=True, stop=True).then_inc(s["o2_done"], 1)

            def scores3(g, columns):
                for col in columns:
                    for b in range(2):
                        pe.matmul(S[:, b, col * N:(col + 1) * N], ident_bf[:, :], mask_mha[:, g.four, :], start=True, stop=False)
                    for b in range(2):
                        h = head_at(4 * b + col)
                        r = slice(DK * (h % 4), DK * (h % 4 + 1))
                        ins = pe.matmul(S[:, b, col * N:(col + 1) * N], qkT[r, g.two, h // 4, :], qkT[r, g.two, 2 + h // 4, :], start=False, stop=True)
                return ins

            def scores3_first(g):
                done(pe, s["qkT_set"], g)
                wait(pe, s["e3T_set"], g.n)
                scores3(g, (0, 1)).then_inc(s["s_half"], 1)

            def scores3_last(g):
                done(pe, s["s_half"], g)
                scores3(g, (2, 3)).then_inc(s["s_done"], 1)

            def norm2_transpose(g):
                done(pe, s["z2_set"], g)
                done(pe, s["en2_set"], g)
                for k in range(KD):
                    ins = pe.transpose(T2[:, k * N:(k + 1) * N], z[:, g.two, 1, k * 128:(k + 1) * 128], ident[:, :])
                ins.then_inc(s["t2_done"], 1)

            def transpose1(g):
                done(pe, s["eTn_set"], g)
                for h in range(H):
                    ins = pe.transpose(ET[:, h * N:(h + 1) * N], eTn[:, g.two, h * N:(h + 1) * N], ident[:, :])
                ins.then_inc(s["et_done"], 1)

            def project_out(g):
                done(pe, s["attT_set"], g)
                for k in range(KD):
                    ins = pe.matmul(WO[:, 0:D], chunks(attT, g)[:, k], wo[:, k, :], start=k == 0, stop=k == KD - 1)
                ins.then_inc(s["wo_done"], 1)

            def norm1_transpose(g):
                done(pe, s["z_set"], g)
                wait(pe, s["qkT_set"], g.n - 2)
                for k in range(KD):
                    ins = pe.transpose(T1[:, k * N:(k + 1) * N], z[:, g.two, 0, k * 128:(k + 1) * 128], ident[:, :])
                ins.then_inc(s["t1_done"], 1)

            def aggregate1(g):
                done(pe, s["en_set"], g)
                done(pe, s["xl_set"], g)
                wait(pe, s["x1_set"], g.n)
                for h in range(H):
                    ins = pe.matmul(O1[:, h * N:(h + 1) * N], xl[:, g.two, h * F:(h + 1) * F], en[:, g.two, h * N:(h + 1) * N], start=True, stop=True)
                ins.then_inc(s["o1_done"], 1)

            steps(pe, lambda graphs: run([
                (project1, A_), (mha_transpose, D_), (project2, B_), (mha_av, D_), (scores2, B_), (scores1, A_), (qk, C_),
                (transpose2, B_), (att_transpose, D_), (scores3_first, C_), (project_v, C_), (aggregate2, B_), (scores3_last, C_), (norm2_transpose, B_),
                (transpose1, A_), (project_out, D_), (norm1_transpose, P_), (aggregate1, A_),
            ], graphs))


_INS = ['x', 'adj', 'L0_gnn_W1', 'L0_gnn_att_src1', 'L0_gnn_att_dst1', 'L0_gnn_b1', 'L0_gnn_W2', 'L0_gnn_att_src2',
        'L0_gnn_att_dst2', 'L0_gnn_b2', 'L1_gnn_Wq', 'L1_gnn_Wk', 'L1_gnn_Wv', 'L1_gnn_Wo']


def kernel(**inputs):
    import numpy as _np
    import concourse.bacc as _bacc
    from concourse import mybir as _mybir
    from concourse.bass_utils import run_bass_kernel_spmd as _run

    nc = _bacc.Bacc("TRN2", target_bir_lowering=False, num_devices=1)
    arrays, args = {}, []
    for name in _INS:
        a = _np.ascontiguousarray(inputs[name])
        arrays[f"in_{name}_dram"] = a
        args.append(nc.dram_tensor(f"in_{name}_dram", a.shape, _mybir.dt.from_np(a.dtype), kind="ExternalInput").ap())
    shape = _np.shape(inputs["x"])
    args.append(nc.dram_tensor("out_dram", shape, _mybir.dt.float32, kind="ExternalOutput").ap())
    gnn_kernel(nc, *args)
    r = _run(nc, [arrays], core_ids=[0])
    return r.results[0]["out_dram"]
```

```python
from contextlib import ExitStack

import concourse.bass as bass
from concourse import mybir

F32 = mybir.dt.float32
BF16 = mybir.dt.bfloat16
F16 = mybir.dt.float16
I32 = mybir.dt.int32
ALU = mybir.AluOpType
ACT = mybir.ActivationFunctionType
AX = mybir.AxisListType

EPS = 1e-5
SLOPE = 0.2
BIG = 1e30
UNROLL = 4
P_, A_, B_, C_, D_ = range(5)
L_ = -1


class Graph:

    def __init__(self, base, unrolled, lag, count):
        self.n = base + (unrolled - lag)
        self.four = (unrolled - lag) % 4
        self.two = (unrolled - lag) % 2
        self.dma = base * 4 + 16 * ((unrolled - lag) // 4 + 1)
        self.active = not isinstance(base, int) or 0 <= self.n < count


def wait(eng, sem, value):
    if not isinstance(value, int) or value > 0:
        eng.wait_ge(sem, value)


def done(eng, sem, g):
    wait(eng, sem, g.n + 1)


def free(eng, sem, g, ring=2):
    wait(eng, sem, g.n + 1 - ring)


def gnn_kernel(nc, x, adj, W1, att_src1, att_dst1, b1, W2, att_src2, att_dst2, b2, Wq, Wk, Wv, Wo, out):
    G, N, D = x.shape
    H, F = att_src1.shape
    HF = H * F
    KD = D // 128
    NH, DK = 8, D // 8
    HALF = HF // 2 + 2 * (H // 2)
    SCALE = float(DK) ** -0.5

    ctx = ExitStack()
    with ctx:
        def sb(name, shape, dt=F32):
            return ctx.enter_context(nc.sbuf_tensor(name, shape, dt))

        def sem(name):
            return ctx.enter_context(nc.semaphore(name))

        ident = sb("ident", [128, 128])
        ident_bf = sb("ident_bf", [128, 128], BF16)
        offdiag = sb("offdiag", [128, 128])
        ones = sb("ones", [128, 128])
        minus_half = sb("minus_half", [128, 1])
        pause = sb("pause", [128, 1])
        w1 = sb("w1", [128, KD, 2, HALF])
        w2 = sb("w2", [128, H, D + 2])
        wqkv = sb("wqkv", [128, KD, 3, D])
        w1_split = sb("w1_split", [128, 2, KD, 2, HALF], F16)
        wqkv_split = sb("wqkv_split", [128, 2, KD, 3, D], F16)
        largest = sb("largest", [128, 5])
        largest_all = sb("largest_all", [128, 5])
        power = sb("power", [128, 5])
        scale = sb("scale", [128, 5])
        q_power = sb("q_power", [128, 2])
        wo = sb("wo", [128, KD, D])
        b1_all = sb("b1_all", [128, HF])
        b2_all = sb("b2_all", [128, D])
        att1 = sb("att1", [128, 2, HF])
        att2 = sb("att2", [128, 2, D])
        prod = sb("prod", [128, 4, HF])

        x_in = sb("x_in", [128, 4, D])
        adj_in = sb("adj_in", [128, 4, N], I32)
        mask_gat = sb("mask_gat", [128, 4, N], BF16)
        mask_mha = sb("mask_mha", [128, 4, N], BF16)
        stats = sb("stats", [128, 2, 2, 6])
        mv = sb("mv", [128, 2, 2, 2])
        var = sb("var", [128, 2, 2])
        rstd = sb("rstd", [128, 2, 2])
        z = sb("z", [128, 2, 2, D])
        hT = sb("hT", [128, 2, 2, D], F16)
        xl = sb("xl", [128, 2, HF])
        ab = sb("ab", [128, 2, 2, 4])
        diag = sb("diag", [128, 2, HF])
        zb = sb("zb", [128, 2, HF])
        lr = sb("lr", [128, 2, HF])
        nmx = sb("nmx", [128, 2, H])
        eT = sb("eT", [128, 2, HF])
        sm = sb("sm", [128, 2, H])
        rs = sb("rs", [128, 2, H])
        eTn = sb("eTn", [128, 2, HF])
        en = sb("en", [128, 2, HF])
        ex = sb("ex", [128, 2, HF])
        ex1 = sb("ex1", [128, 2, HF])
        h1T = sb("h1T", [128, 2, HF])
        xl2 = sb("xl2", [128, 2, D])
        ab2 = sb("ab2", [128, 2, 2])
        diag2 = sb("diag2", [128, 2, N])
        zb2 = sb("zb2", [128, 2, N])
        lr2 = sb("lr2", [128, 2, N])
        nmx2 = sb("nmx2", [128, 2, 1])
        eT2 = sb("eT2", [128, 2, N])
        sm2 = sb("sm2", [128, 2, 1])
        rs2 = sb("rs2", [128, 2, 1])
        en2 = sb("en2", [128, 2, N])
        x1 = sb("x1", [128, 4, D])
        h2T = sb("h2T", [128, 2, 2, D], F16)
        qkT = sb("qkT", [128, 2, 4, N])
        vv = sb("vv", [128, 2, 2, NH, DK + 1], F16)
        nmx3 = sb("nmx3", [128, 2, NH])
        e3 = sb("e3", [128, 2, NH, N])
        e3T = sb("e3T", [128, 2, 2, NH, N], F16)
        rs3 = sb("rs3", [128, 2, NH])
        att = sb("att", [128, 2, D])
        attT = sb("attT", [128, 2, D])
        x_out = sb("x_out", [128, 4, D])

        bank = ctx.enter_context(nc.psum_tensor("bank", [128, 8, 512], F32))
        XL, EM, X2, AV, Z2, Z = bank[:, 0:2, :], bank[:, 2:4, :], bank[:, 4], bank[:, 5], bank[:, 6], bank[:, 7]
        QK, ET2, T3, V, O2, S = bank[:, 0], bank[:, 4], bank[:, 5], bank[:, 1], bank[:, 6], bank[:, 2:4, :]
        T2, ET, WO, T1, O1 = bank[:, 7], bank[:, 7], bank[:, 5], bank[:, 0], bank[:, 6]

        names = """ident_set ones_set const_set weights_in att_in w1_prod w1_set w2_prod w2_set largest_set largest_all_set power_set scale_set q_power_set wo_set split_high split_low
            masks_set stats_set mv_set var_set rstd_set z_set
            stats2_set mv2_set var2_set rstd2_set z2_set
            t1_done hT_high hT_set xl_done xl_set ab_set diag_set zsc_done zb_set lr_set nmx_set eT_set rs_set eTn_set
            et_done en_set o1_done ex_set ex1_set h1T_set x2_done xl2_set ab2_set diag2_set zsc2_done zb2_set lr2_set
            nmx2_set eT2_set rs2_set et2_done en2_set o2_done x1_set t2_done h2T_high h2T_set qk_done qkT_set v_done
            vv_high vv_set s_half s_done nmx3_set e3_set em_done e3T_high e3T_set av_done rs3_set att_set t3_done attT_set wo_done
            x_out_set""".split()
        s = {n: sem(n) for n in names}
        x_here = [sem(f"x_here{i}") for i in range(4)]
        adj_here = [sem(f"adj_here{i}") for i in range(4)]
        stored = [sem(f"stored{i}") for i in range(4)]

        def head_at(j):
            return j // 4 + (0, 4, 2, 6)[j % 4]

        def steps(eng, body, peeled=0):
            def step(base, unrolled):
                body({lag: Graph(base, unrolled, lag, G) for lag in (L_, P_, A_, B_, C_, D_)})

            for t in range(2 * UNROLL):
                step(t - t % UNROLL, t % UNROLL)
            with eng.Fori(2 * UNROLL, G - peeled - UNROLL + 1, UNROLL) as t:
                for u in range(UNROLL):
                    step(t, u)
            for t in range(G - peeled, G + D_):
                step(t - t % UNROLL, t % UNROLL)

        def run(body_functions, graphs):
            for function, phase in body_functions:
                if graphs[phase].active:
                    function(graphs[phase])

        block = ctx.enter_context(nc.Block())

        @block.sync
        def _(sp):
            for k in range(KD):
                sp.dma_start(w1[:, k, :, 0:HF // 2], W1[k * 128:(k + 1) * 128, :].rearrange("p (a c) -> p a c", a=2)).then_inc(s["weights_in"], 16)
            for k in range(2):
                sp.dma_start(att1[:, k, :], (att_src1, att_dst1)[k].rearrange("h f -> (h f)").partition_broadcast(128)).then_inc(s["att_in"], 16)
                sp.dma_start(att2[:, k, :], (att_src2, att_dst2)[k].rearrange("h f -> (h f)").partition_broadcast(128)).then_inc(s["att_in"], 16)
            sp.dma_start(b1_all[:, :], b1.partition_broadcast(128)).then_inc(s["weights_in"], 16)
            sp.dma_start(b2_all[:, :], b2.partition_broadcast(128)).then_inc(s["weights_in"], 16)
            sp.dma_start(w2[:, :, 0:D], W2.rearrange("(k p) n -> p k n", p=128)).then_inc(s["weights_in"], 16)
            sp.dma_start(wqkv[:, :, 0, :], Wq.rearrange("(k p) n -> p k n", p=128)).then_inc(s["weights_in"], 16)
            sp.dma_start(wqkv[:, :, 1, :], Wk.rearrange("(k p) n -> p k n", p=128)).then_inc(s["weights_in"], 16)
            sp.dma_start(wqkv[:, :, 2, :], Wv.rearrange("(k p) n -> p k n", p=128)).then_inc(s["weights_in"], 16)
            sp.dma_start(wo[:, :, :], Wo.rearrange("(k p) n -> p k n", p=128)).then_inc(s["weights_in"], 16)

            def load(g):
                free(sp, s["x1_set"], g, 4)
                sp.dma_start(x_in[:, g.four, :], x[bass.ds(g.n, 1)].rearrange("a n d -> (a n) d")).then_inc(x_here[g.four], 16)
                free(sp, s["masks_set"], g, 4)
                sp.dma_start(adj_in[:, g.four, :], adj[bass.ds(g.n, 1)].rearrange("a n d -> (a n) d")).then_inc(adj_here[g.four], 16)

            def store(g):
                done(sp, s["x_out_set"], g)
                sp.dma_start(out[bass.ds(g.n, 1)].rearrange("a n d -> (a n) d"), x_out[:, g.four, :]).then_inc(stored[g.four], 16)

            load(Graph(0, 0, 0, G))
            steps(sp, lambda graphs: run([(load, L_), (store, D_)], graphs), peeled=UNROLL)
            for n in range(4):
                sp.wait_ge(stored[n], 16 * (G // 4))

        @block.gpsimd
        def _(pool):
            pool.memset(ident[:, :], 0.0).then_inc(s["ident_set"], 1)
            pool.memset(offdiag[:, :], -BIG).then_inc(s["ident_set"], 1)
            pool.memset(ones[:, :], 1.0).then_inc(s["ones_set"], 1)
            pool.memset(minus_half[:, :], -0.5).then_inc(s["ones_set"], 1)
            pool.memset(vv[:, :, 0, :, DK:DK + 1], 1.0).then_inc(s["ones_set"], 1)
            pool.wait_ge(s["ident_set"], 2)
            for tile, fill in ((ident, 1.0), (offdiag, 0.0)):
                pool.affine_select(out=tile[:, :], in_=tile[:, :], compare_op=ALU.not_equal, fill=fill, base=0,
                                   pattern=[[-1, 128]], channel_multiplier=1).then_inc(s["ident_set"], 1)
            pool.wait_ge(s["ident_set"], 4)
            pool.tensor_copy(ident_bf[:, :], ident[:, :]).then_inc(s["ident_set"], 1)

            pool.wait_ge(s["largest_set"], 4)
            pool.partition_all_reduce(largest_all[:, :], largest[:, :], 128, bass.bass_isa.ReduceOp.max).then_inc(s["largest_all_set"], 1)

            def diagonals(g):
                done(pool, s["ab_set"], g)
                free(pool, s["zsc_done"], g)
                pool.tensor_tensor(
                    diag[:, g.two, :].rearrange("p (a h n) -> p a h n", a=2, h=2),
                    ident[:, :].unsqueeze(1).unsqueeze(1).to_broadcast((128, 2, 2, N)),
                    ab[:, g.two, :, 0:2].unsqueeze(3).to_broadcast((128, 2, 2, N)), ALU.mult).then_inc(s["diag_set"], 1)

            def diagonal2(g):
                done(pool, s["ab2_set"], g)
                free(pool, s["zsc2_done"], g)
                pool.tensor_tensor(diag2[:, g.two, :], ident[:, :], ab2[:, g.two, 0:1].to_broadcast((128, N)), ALU.mult).then_inc(s["diag2_set"], 1)

            def normalise(g):
                done(pool, s["rs_set"], g)
                done(pool, s["eT_set"], g)
                free(pool, s["et_done"], g)
                pool.tensor_tensor(eTn[:, g.two, :].rearrange("p (h n) -> p h n", h=H), eT[:, g.two, :].rearrange("p (h n) -> p h n", h=H),
                                   rs[:, g.two, :].unsqueeze(2).to_broadcast((128, H, N)), ALU.mult).then_inc(s["eTn_set"], 1)

            def rsqrt(g, which, var_set, free_sem, rstd_set):
                done(pool, s[var_set], g)
                free(pool, s[free_sem], g)
                pool.tensor_tensor(rstd[:, g.two, which:which + 1], var[:, g.two, which:which + 1], minus_half[:, :], ALU.pow).then_inc(s[rstd_set], 1)

            def rsqrt1(g):
                rsqrt(g, 0, "var_set", "z_set", "rstd_set")

            def rsqrt2(g):
                rsqrt(g, 1, "var2_set", "z2_set", "rstd2_set")

            steps(pool, lambda graphs: run([(diagonals, A_), (diagonal2, B_), (rsqrt1, P_), (normalise, A_), (rsqrt2, B_)], graphs))

        @block.scalar
        def _(act):
            act.wait_ge(s["q_power_set"], 2)
            def relu1(g):
                done(act, s["t1_done"], g)
                free(act, s["xl_done"], g)
                act.activation(hT[:, g.two, 0, :], T1[:, 0:D], ACT.Relu).then_inc(s["hT_high"], 1)

            def gat1_exp(g):
                done(act, s["nmx_set"], g)
                free(act, s["eTn_set"], g)
                for h in range(H):
                    ins = act.activation(eT[:, g.two, h * N:(h + 1) * N], lr[:, g.two, h * N:(h + 1) * N], ACT.Exp,
                                         bias=nmx[:, g.two, h:h + 1], accum_out=sm[:, g.two, h:h + 1])
                ins.then_inc(s["eT_set"], 1)

            def gat1_copy(g):
                done(act, s["et_done"], g)
                free(act, s["o1_done"], g)
                act.activation(en[:, g.two, :], ET[:, :], ACT.Copy).then_inc(s["en_set"], 1)

            def elu_exp(g):
                done(act, s["o1_done"], g)
                free(act, s["ex1_set"], g)
                act.activation(ex[:, g.two, :], O1[:, :], ACT.Exp).then_inc(s["ex_set"], 1)
                done(act, s["ex_set"], g)
                free(act, s["h1T_set"], g)
                act.activation(ex1[:, g.two, :], ex[:, g.two, :], ACT.Relu, bias=1.0, scale=-1.0).then_inc(s["ex1_set"], 1)

            def gat2_exp(g):
                done(act, s["nmx2_set"], g)
                free(act, s["et2_done"], g)
                free(act, s["rs2_set"], g)
                act.activation(eT2[:, g.two, :], lr2[:, g.two, :], ACT.Exp, bias=nmx2[:, g.two, :],
                               accum_out=sm2[:, g.two, :]).then_inc(s["eT2_set"], 1)

            def gat2_copy(g):
                done(act, s["et2_done"], g)
                free(act, s["o2_done"], g)
                act.activation(en2[:, g.two, :], ET2[:, 0:N], ACT.Copy).then_inc(s["en2_set"], 1)

            def relu2(g):
                done(act, s["t2_done"], g)
                free(act, s["v_done"], g)
                act.activation(h2T[:, g.two, 0, :], T2[:, 0:D], ACT.Relu).then_inc(s["h2T_high"], 1)

            def qk_copy(g):
                done(act, s["qk_done"], g)
                free(act, s["s_done"], g)
                act.activation(qkT[:, g.two, 0:2, :], QK[:, 0:2 * N].rearrange("p (c n) -> p c n", c=2), ACT.Copy, scale=q_power[:, 1:2])
                act.activation(qkT[:, g.two, 2:4, :], QK[:, 2 * N:].rearrange("p (c n) -> p c n", c=2), ACT.Copy).then_inc(s["qkT_set"], 1)

            def v_copy(g):
                done(act, s["v_done"], g)
                free(act, s["av_done"], g)
                act.activation(vv[:, g.two, 0, :, 0:DK], V[:, 0:D].rearrange("p (h c) -> p h c", h=NH), ACT.Copy).then_inc(s["vv_high"], 1)

            def mha_exp(g):
                done(act, s["nmx3_set"], g)
                free(act, s["em_done"], g)
                for h in range(NH):
                    ins = act.activation(e3[:, g.two, h, :], S[:, h // 4, (h % 4) * N:(h % 4 + 1) * N], ACT.Exp,
                                         bias=nmx3[:, g.two, h:h + 1])
                ins.then_inc(s["e3_set"], 1)

            def mha_copy(g):
                done(act, s["em_done"], g)
                free(act, s["av_done"], g)
                act.activation(e3T[:, g.two, 0, :, :], EM.rearrange("p b (h n) -> p (b h) n", h=4), ACT.Copy).then_inc(s["e3T_high"], 1)

            def att_copy(g):
                done(act, s["t3_done"], g)
                free(act, s["wo_done"], g)
                act.activation(attT[:, g.two, :], T3[:, 0:D], ACT.Copy).then_inc(s["attT_set"], 1)

            steps(act, lambda graphs: run([
                (relu1, A_), (mha_exp, D_), (elu_exp, B_), (mha_copy, D_), (relu2, C_), (gat2_exp, B_), (qk_copy, C_),
                (gat2_copy, B_), (gat1_exp, A_), (att_copy, D_), (v_copy, C_), (gat1_copy, A_),
            ], graphs))

        @block.vector
        def _(dve):
            dve.wait_ge(s["weights_in"], 16 * 9)
            dve.wait_ge(s["att_in"], 16 * 4)
            for k in range(KD):
                for j in range(2):
                    dve.tensor_tensor(prod[:, 2 * k + j, :].rearrange("p (a c) -> p a c", a=2), w1[:, k, :, 0:HF // 2],
                                      att1[:, j, :].rearrange("p (a c) -> p a c", a=2), ALU.mult).then_inc(s["w1_prod"], 1)
            dve.wait_ge(s["w1_prod"], 2 * KD)
            for k in range(KD):
                for j in range(2):
                    dve.tensor_reduce(w1[:, k, :, HF // 2 + 2 * j:HF // 2 + 2 * j + 2],
                                      prod[:, 2 * k + j, :].rearrange("p (a h f) -> p a h f", a=2, h=2), AX.X, ALU.add).then_inc(s["w1_set"], 1)
            dve.wait_ge(s["w1_set"], 2 * KD)
            for j in range(2):
                for half in range(2):
                    dve.tensor_tensor(prod[:, 2 * j + half, :].rearrange("p (a c) -> p a c", a=2), w2[:, 2 * half:2 * half + 2, 0:D],
                                      att2[:, j, :].unsqueeze(1).to_broadcast((128, 2, D)), ALU.mult).then_inc(s["w2_prod"], 1)
            dve.wait_ge(s["w2_prod"], 4)
            for j in range(2):
                dve.tensor_reduce(w2[:, :, D + j:D + j + 1], prod[:, 2 * j:2 * j + 2, :].rearrange("p b (a c) -> p b a c", a=2),
                                  AX.X, ALU.add).then_inc(s["w2_set"], 1)

            high = slice(0, HF // 2)
            columns = slice(HF // 2, HALF)
            dve.wait_ge(s["w1_set"], 2 * KD)
            for i, part in enumerate((w1[:, :, :, high], w1[:, :, :, columns])):
                dve.tensor_reduce(largest[:, i:i + 1], part, AX.XYZ, ALU.max, apply_absolute_value=True).then_inc(s["largest_set"], 1)
            dve.memset(power[:, :], 0.0).then_inc(s["largest_set"], 1)
            dve.tensor_reduce(largest[:, 2:5], wqkv[:, :, :, :].rearrange("p k m n -> p m k n"), AX.XY, ALU.max,
                              apply_absolute_value=True).then_inc(s["largest_set"], 1)
            dve.wait_ge(s["largest_all_set"], 1)
            dve.tensor_scalar(power[:, :], largest_all[:, :], 2.0 ** -60, None, ALU.max).then_inc(s["power_set"], 1)
            dve.wait_ge(s["power_set"], 1)
            bits = power[:, :].bitcast(I32)
            dve.tensor_scalar(bits, bits, 0x7f800000, None, ALU.bitwise_and).then_inc(s["power_set"], 1)
            dve.wait_ge(s["power_set"], 2)
            dve.tensor_scalar(scale[:, :].bitcast(I32), bits, -1.0, float(254 << 23), ALU.mult, ALU.add).then_inc(s["scale_set"], 1)
            dve.tensor_tensor(q_power[:, 0:1], power[:, 2:3], power[:, 3:4], ALU.mult).then_inc(s["q_power_set"], 1)
            dve.wait_ge(s["q_power_set"], 1)
            dve.tensor_scalar(q_power[:, 1:2], q_power[:, 0:1], SCALE, None, ALU.mult).then_inc(s["q_power_set"], 1)
            dve.tensor_scalar(wo[:, :, :], wo[:, :, :], power[:, 4:5], None, ALU.mult).then_inc(s["wo_set"], 1)
            dve.wait_ge(s["scale_set"], 1)
            parts = [(w1[:, :, :, high], w1_split[:, :, :, :, high], 0), (w1[:, :, :, columns], w1_split[:, :, :, :, columns], 1)]
            parts += [(wqkv[:, :, m, :], wqkv_split[:, :, :, m, :], 2 + m) for m in range(3)]
            for part, split, i in parts:
                dve.tensor_scalar(split[:, 0], part, scale[:, i:i + 1], None, ALU.mult).then_inc(s["split_high"], 1)
            dve.wait_ge(s["split_high"], 5)
            for part, split, i in parts:
                for k in range(KD):
                    dve.scalar_tensor_tensor(out=split[:, 1, k], in0=part[:, k], scalar=scale[:, i:i + 1], in1=split[:, 0, k],
                                             op0=ALU.mult, op1=ALU.subtract).then_inc(s["split_low"], 1)

            def remainder(out_, in_, high_, sem_):
                dve.scalar_tensor_tensor(out=out_, in0=in_, scalar=0.0, in1=high_, op0=ALU.max, op1=ALU.subtract).then_inc(s[sem_], 1)

            def relu1_low(g):
                done(dve, s["hT_high"], g)
                free(dve, s["xl_done"], g)
                remainder(hT[:, g.two, 1, :], T1[:, 0:D], hT[:, g.two, 0, :], "hT_set")

            def relu2_low(g):
                done(dve, s["h2T_high"], g)
                free(dve, s["v_done"], g)
                remainder(h2T[:, g.two, 1, :], T2[:, 0:D], h2T[:, g.two, 0, :], "h2T_set")

            def mha_low(g):
                done(dve, s["e3T_high"], g)
                free(dve, s["av_done"], g)
                dve.tensor_tensor(e3T[:, g.two, 1, :, :], EM.rearrange("p b (h n) -> p (b h) n", h=4), e3T[:, g.two, 0, :, :],
                                  ALU.subtract).then_inc(s["e3T_set"], 1)

            def moments(g, which, src, stats_set, mv_set, var_set):
                dve.bn_stats(stats[:, g.two, which, :], src).then_inc(s[stats_set], 1)
                done(dve, s[stats_set], g)
                dve.memset(pause[:, :], 0.0)
                dve.bn_aggr(mv[:, g.two, which, :], stats[:, g.two, which, :]).then_inc(s[mv_set], 1)
                done(dve, s[mv_set], g)
                dve.tensor_scalar(var[:, g.two, which:which + 1], mv[:, g.two, which, 1:2], EPS, None, ALU.add).then_inc(s[var_set], 1)

            def normed(g, which, src, rstd_set, free_sem, z_set):
                done(dve, s[rstd_set], g)
                free(dve, s[free_sem], g)
                dve.tensor_scalar(z[:, g.two, which, :], src, mv[:, g.two, which, 0:1], rstd[:, g.two, which:which + 1],
                                  ALU.subtract, ALU.mult).then_inc(s[z_set], 1)

            def masks(g):
                dve.wait_ge(adj_here[g.four], g.dma)
                free(dve, s["s_done"], g, 4)
                dve.tensor_scalar(mask_mha[:, g.four, :], adj_in[:, g.four, :], 0.0, -BIG, ALU.is_equal, ALU.mult)
                dve.scalar_tensor_tensor(out=mask_gat[:, g.four, :], in0=adj_in[:, g.four, :], scalar=0.0, in1=offdiag[:, :],
                                         op0=ALU.is_le, op1=ALU.mult).then_inc(s["masks_set"], 1)

            def norm1_moments(g):
                dve.wait_ge(x_here[g.four], g.dma)
                moments(g, 0, x_in[:, g.four, :], "stats_set", "mv_set", "var_set")

            def norm1_apply(g):
                normed(g, 0, x_in[:, g.four, :], "rstd_set", "t1_done", "z_set")

            def elu(g):
                done(dve, s["ex1_set"], g)
                free(dve, s["x2_done"], g)
                dve.scalar_tensor_tensor(out=h1T[:, g.two, :], in0=ex1[:, g.two, :], scalar=-1.0, in1=O1[:, :],
                                         op0=ALU.mult, op1=ALU.max).then_inc(s["h1T_set"], 1)

            def xl_evac(g):
                done(dve, s["xl_done"], g)
                free(dve, s["diag_set"], g)
                dve.tensor_scalar(ab[:, g.two, :, :], XL[:, :, HF // 2:HALF], power[:, 1:2], None, ALU.mult).then_inc(s["ab_set"], 1)
                free(dve, s["o1_done"], g)
                dve.scalar_tensor_tensor(out=xl[:, g.two, :].rearrange("p (a c) -> p a c", a=2), in0=XL[:, :, 0:HF // 2],
                                         scalar=power[:, 0:1], in1=b1_all[:, :].rearrange("p (a c) -> p a c", a=2),
                                         op0=ALU.mult, op1=ALU.add).then_inc(s["xl_set"], 1)

            def xl2_evac(g):
                done(dve, s["x2_done"], g)
                dve.tensor_copy(ab2[:, g.two, :], X2[:, D:D + 2]).then_inc(s["ab2_set"], 1)
                free(dve, s["o2_done"], g)
                dve.tensor_tensor(xl2[:, g.two, :], X2[:, 0:D], b2_all[:, :], ALU.add).then_inc(s["xl2_set"], 1)

            def att_norm(g):
                done(dve, s["av_done"], g)
                av = AV[:, 0:NH * (DK + 1)].rearrange("p (h c) -> p h c", h=NH)
                dve.reciprocal(rs3[:, g.two, :].unsqueeze(2), av[:, :, DK:DK + 1]).then_inc(s["rs3_set"], 1)
                done(dve, s["rs3_set"], g)
                free(dve, s["t3_done"], g)
                dve.scalar_tensor_tensor(out=att[:, g.two, :].rearrange("p (h c) -> p h c", h=NH), in0=av[:, :, 0:DK], scalar=0.0,
                                         in1=rs3[:, g.two, :].unsqueeze(2).to_broadcast((128, NH, DK)),
                                         op0=ALU.max, op1=ALU.mult).then_inc(s["att_set"], 1)

            def gat2_scores(g):
                done(dve, s["zsc2_done"], g)
                dve.tensor_scalar(zb2[:, g.two, :], Z2[:, 0:N], ab2[:, g.two, 1:2], None, ALU.add).then_inc(s["zb2_set"], 1)
                done(dve, s["zb2_set"], g)
                free(dve, s["eT2_set"], g)
                dve.scalar_tensor_tensor(out=lr2[:, g.two, :], in0=zb2[:, g.two, :], scalar=SLOPE, in1=zb2[:, g.two, :],
                                         op0=ALU.mult, op1=ALU.max).then_inc(s["lr2_set"], 1)
                done(dve, s["lr2_set"], g)
                dve.tensor_reduce(nmx2[:, g.two, :], lr2[:, g.two, :], AX.X, ALU.max, negate=True).then_inc(s["nmx2_set"], 1)

            def gat1_scores(g):
                done(dve, s["zsc_done"], g)
                dve.tensor_tensor(zb[:, g.two, :].rearrange("p (a h n) -> p a h n", a=2, h=2),
                                  Z.rearrange("p (a h n) -> p a h n", a=2, h=2),
                                  ab[:, g.two, :, 2:4].unsqueeze(3).to_broadcast((128, 2, 2, N)), ALU.add).then_inc(s["zb_set"], 1)
                done(dve, s["zb_set"], g)
                free(dve, s["eT_set"], g)
                dve.scalar_tensor_tensor(out=lr[:, g.two, :], in0=zb[:, g.two, :], scalar=SLOPE, in1=zb[:, g.two, :],
                                         op0=ALU.mult, op1=ALU.max).then_inc(s["lr_set"], 1)
                done(dve, s["lr_set"], g)
                dve.tensor_reduce(nmx[:, g.two, :], lr[:, g.two, :].rearrange("p (h n) -> p h n", h=H), AX.X, ALU.max,
                                  negate=True).then_inc(s["nmx_set"], 1)

            def gat2_recip(g):
                done(dve, s["eT2_set"], g)
                dve.reciprocal(rs2[:, g.two, :], sm2[:, g.two, :]).then_inc(s["rs2_set"], 1)

            def v_low(g):
                done(dve, s["vv_high"], g)
                free(dve, s["av_done"], g)
                dve.tensor_tensor(vv[:, g.two, 1, :, 0:DK], V[:, 0:D].rearrange("p (h c) -> p h c", h=NH), vv[:, g.two, 0, :, 0:DK],
                                  ALU.subtract).then_inc(s["vv_set"], 1)

            def residual1(g):
                done(dve, s["o2_done"], g)
                done(dve, s["rs2_set"], g)
                dve.scalar_tensor_tensor(out=x1[:, g.four, :], in0=O2[:, 0:D], scalar=rs2[:, g.two, :], in1=x_in[:, g.four, :],
                                         op0=ALU.mult, op1=ALU.add).then_inc(s["x1_set"], 1)

            def norm2_moments(g):
                done(dve, s["x1_set"], g)
                moments(g, 1, x1[:, g.four, :], "stats2_set", "mv2_set", "var2_set")

            def norm2_apply(g):
                normed(g, 1, x1[:, g.four, :], "rstd2_set", "t2_done", "z2_set")

            def gat1_recip(g):
                done(dve, s["eT_set"], g)
                dve.reciprocal(rs[:, g.two, :], sm[:, g.two, :]).then_inc(s["rs_set"], 1)

            def mha_max(g):
                done(dve, s["s_done"], g)
                free(dve, s["e3_set"], g)
                dve.tensor_reduce(nmx3[:, g.two, :], S.rearrange("p b (h n) -> p (b h) n", h=4), AX.X, ALU.max,
                                  negate=True).then_inc(s["nmx3_set"], 1)

            def residual2(g):
                done(dve, s["wo_done"], g)
                if not isinstance(g.n, int) or g.n >= 4:
                    dve.wait_ge(stored[g.four], g.dma - 16)
                dve.tensor_tensor(x_out[:, g.four, :], WO[:, 0:D], x1[:, g.four, :], ALU.add).then_inc(s["x_out_set"], 1)

            dve.wait_ge(s["ident_set"], 5)
            steps(dve, lambda graphs: run([
                (relu1_low, A_), (norm1_moments, P_), (masks, P_), (xl_evac, A_), (elu, B_), (mha_low, D_),
                (relu2_low, C_), (xl2_evac, B_), (att_norm, D_), (gat2_scores, B_), (gat1_scores, A_), (gat2_recip, B_),
                (norm1_apply, P_), (gat1_recip, A_), (residual1, B_), (v_low, C_), (norm2_moments, B_), (mha_max, C_),
                (norm2_apply, B_), (residual2, D_),
            ], graphs))

        @block.tensor
        def _(pe):
            pe.wait_ge(s["weights_in"], 16 * 9)
            pe.wait_ge(s["ident_set"], 5)
            pe.wait_ge(s["ones_set"], 3)
            pe.wait_ge(s["w1_set"], 2 * KD)
            pe.wait_ge(s["w2_set"], 2)
            pe.wait_ge(s["wo_set"], 1)
            pe.wait_ge(s["split_low"], 5 * KD)

            def chunks(tile):
                return tile.rearrange("p (k n) -> p k n", n=128)

            SPLIT = ((0, 0), (0, 1), (1, 0))

            def split_matmul(out_, groups):
                pairs = [p for group in groups for p in group]
                for n, (left, right) in enumerate(pairs):
                    ins = pe.matmul(out_, left, right, start=n == 0, stop=n == len(pairs) - 1)
                return ins

            def project1(g):
                done(pe, s["hT_set"], g)
                free(pe, s["vv_set"], g, 3)
                for a in range(2):
                    ins = split_matmul(XL[:, a, 0:HALF], [
                        [(chunks(hT[:, g.two, i, :])[:, k], w1_split[:, j, k, a, :]) for i, j in SPLIT] for k in range(KD)])
                ins.then_inc(s["xl_done"], 1)

            def mha_transpose(g):
                done(pe, s["e3_set"], g)
                for h in range(NH):
                    ins = pe.transpose(EM[:, h // 4, (h % 4) * N:(h % 4 + 1) * N], e3[:, g.two, h, :], ident[:, :])
                ins.then_inc(s["em_done"], 1)

            def project2(g):
                done(pe, s["h1T_set"], g)
                for k in range(H):
                    ins = pe.matmul(X2[:, 0:D + 2], h1T[:, g.two, k * F:(k + 1) * F], w2[:, k, :], start=k == 0, stop=k == H - 1)
                ins.then_inc(s["x2_done"], 1)

            def mha_av(g):
                done(pe, s["e3T_set"], g)
                done(pe, s["vv_set"], g)
                free(pe, s["x_out_set"], g, 1)
                for j in range(NH):
                    h = head_at(j)
                    o = h * (DK + 1)
                    pe.matmul(AV[:, o:o + DK + 1], e3T[:, g.two, 0, j, :], vv[:, g.two, 0, h, :], start=True, stop=False)
                    pe.matmul(AV[:, o:o + DK], e3T[:, g.two, 0, j, :], vv[:, g.two, 1, h, 0:DK], start=False, stop=False)
                    ins = pe.matmul(AV[:, o:o + DK + 1], e3T[:, g.two, 1, j, :], vv[:, g.two, 0, h, :], start=False, stop=True)
                ins.then_inc(s["av_done"], 1)

            def scores2(g):
                done(pe, s["diag2_set"], g)
                done(pe, s["h1T_set"], g)
                pe.matmul(Z2[:, 0:N], ones[:, :], diag2[:, g.two, :], start=True, stop=False)
                pe.matmul(Z2[:, 0:N], mask_gat[:, g.four, :], ident_bf[:, :], start=False, stop=True).then_inc(s["zsc2_done"], 1)

            def scores1(g):
                done(pe, s["diag_set"], g)
                done(pe, s["masks_set"], g)
                free(pe, s["h2T_set"], g, 2)
                pe.matmul(Z[:, :], ones[:, :], diag[:, g.two, :], start=True, stop=False)
                pe.matmul(Z[:, :], mask_gat[:, g.four, :], ident_bf[:, :].unsqueeze(1).to_broadcast((128, H, N)),
                          start=False, stop=True).then_inc(s["zsc_done"], 1)

            def qk(g):
                done(pe, s["h2T_set"], g)
                wait(pe, s["xl_set"], min(g.n + 3, G) if isinstance(g.n, int) else g.n + 3)
                for c in range(4):
                    ins = split_matmul(QK[:, c * N:(c + 1) * N], [
                        [(wqkv_split[:, i, k, c // 2, (c % 2) * 128:(c % 2 + 1) * 128], chunks(h2T[:, g.two, j, :])[:, k]) for i, j in SPLIT]
                        for k in range(KD)])
                ins.then_inc(s["qk_done"], 1)

            def transpose2(g):
                done(pe, s["eT2_set"], g)
                done(pe, s["xl2_set"], g)
                pe.transpose(ET2[:, 0:N], eT2[:, g.two, :], ident[:, :]).then_inc(s["et2_done"], 1)

            def att_transpose(g):
                done(pe, s["att_set"], g)
                for k in range(KD):
                    ins = pe.transpose(T3[:, k * N:(k + 1) * N], att[:, g.two, k * 128:(k + 1) * 128], ident[:, :])
                ins.then_inc(s["t3_done"], 1)

            def project_v(g):
                split_matmul(V[:, 0:D], [
                    [(chunks(h2T[:, g.two, i, :])[:, k], wqkv_split[:, j, k, 2, :]) for i, j in SPLIT] for k in range(KD)]).then_inc(s["v_done"], 1)

            def aggregate2(g):
                done(pe, s["en2_set"], g)
                pe.matmul(O2[:, 0:D], en2[:, g.two, :], xl2[:, g.two, :], start=True, stop=True).then_inc(s["o2_done"], 1)

            def scores3(g, columns):
                for col in columns:
                    for b in range(2):
                        pe.matmul(S[:, b, col * N:(col + 1) * N], ident_bf[:, :], mask_mha[:, g.four, :], start=True, stop=False)
                    for b in range(2):
                        h = head_at(4 * b + col)
                        r = slice(DK * (h % 4), DK * (h % 4 + 1))
                        ins = pe.matmul(S[:, b, col * N:(col + 1) * N], qkT[r, g.two, h // 4, :], qkT[r, g.two, 2 + h // 4, :], start=False, stop=True)
                return ins

            def scores3_first(g):
                done(pe, s["qkT_set"], g)
                wait(pe, s["e3T_set"], g.n)
                scores3(g, (0, 1)).then_inc(s["s_half"], 1)

            def scores3_last(g):
                done(pe, s["s_half"], g)
                scores3(g, (2, 3)).then_inc(s["s_done"], 1)

            def norm2_transpose(g):
                done(pe, s["z2_set"], g)
                for k in range(KD):
                    ins = pe.transpose(T2[:, k * N:(k + 1) * N], z[:, g.two, 1, k * 128:(k + 1) * 128], ident[:, :])
                ins.then_inc(s["t2_done"], 1)

            def transpose1(g):
                done(pe, s["eTn_set"], g)
                for h in range(H):
                    ins = pe.transpose(ET[:, h * N:(h + 1) * N], eTn[:, g.two, h * N:(h + 1) * N], ident[:, :])
                ins.then_inc(s["et_done"], 1)

            def project_out(g):
                done(pe, s["attT_set"], g)
                for k in range(KD):
                    ins = pe.matmul(WO[:, 0:D], chunks(attT[:, g.two, :])[:, k], wo[:, k, :], start=k == 0, stop=k == KD - 1)
                ins.then_inc(s["wo_done"], 1)

            def norm1_transpose(g):
                done(pe, s["z_set"], g)
                wait(pe, s["qkT_set"], g.n - 2)
                for k in range(KD):
                    ins = pe.transpose(T1[:, k * N:(k + 1) * N], z[:, g.two, 0, k * 128:(k + 1) * 128], ident[:, :])
                ins.then_inc(s["t1_done"], 1)

            def aggregate1(g):
                done(pe, s["en_set"], g)
                done(pe, s["xl_set"], g)
                wait(pe, s["x1_set"], g.n)
                for h in range(H):
                    ins = pe.matmul(O1[:, h * N:(h + 1) * N], xl[:, g.two, h * F:(h + 1) * F], en[:, g.two, h * N:(h + 1) * N], start=True, stop=True)
                ins.then_inc(s["o1_done"], 1)

            steps(pe, lambda graphs: run([
                (project1, A_), (mha_transpose, D_), (project2, B_), (mha_av, D_), (scores2, B_), (scores1, A_),
                (qk, C_), (transpose2, B_), (att_transpose, D_), (project_v, C_), (scores3_first, C_), (aggregate2, B_),
                (scores3_last, C_), (transpose1, A_), (project_out, D_), (norm1_transpose, P_), (aggregate1, A_),
                (norm2_transpose, B_),
            ], graphs))


_INS = ['x', 'adj', 'L0_gnn_W1', 'L0_gnn_att_src1', 'L0_gnn_att_dst1', 'L0_gnn_b1', 'L0_gnn_W2', 'L0_gnn_att_src2',
        'L0_gnn_att_dst2', 'L0_gnn_b2', 'L1_gnn_Wq', 'L1_gnn_Wk', 'L1_gnn_Wv', 'L1_gnn_Wo']


def kernel(**inputs):
    import numpy as _np
    import concourse.bacc as _bacc
    from concourse import mybir as _mybir
    from concourse.bass_utils import run_bass_kernel_spmd as _run

    nc = _bacc.Bacc("TRN2", target_bir_lowering=False, num_devices=1)
    arrays, args = {}, []
    for name in _INS:
        a = _np.ascontiguousarray(inputs[name])
        arrays[f"in_{name}_dram"] = a
        args.append(nc.dram_tensor(f"in_{name}_dram", a.shape, _mybir.dt.from_np(a.dtype), kind="ExternalInput").ap())
    shape = _np.shape(inputs["x"])
    args.append(nc.dram_tensor("out_dram", shape, _mybir.dt.float32, kind="ExternalOutput").ap())
    gnn_kernel(nc, *args)
    r = _run(nc, [arrays], core_ids=[0])
    return r.results[0]["out_dram"]
```

```python
from contextlib import ExitStack

import concourse.bass as bass
from concourse import mybir

F32 = mybir.dt.float32
BF16 = mybir.dt.bfloat16
F16 = mybir.dt.float16
I32 = mybir.dt.int32
ALU = mybir.AluOpType
ACT = mybir.ActivationFunctionType
AX = mybir.AxisListType

EPS = 1e-5
SLOPE = 0.2
BIG = 1e30
UNROLL = 4
P_, A_, B_, C_, D_ = range(5)
L_ = -1


class Graph:

    def __init__(self, base, unrolled, lag, count):
        self.n = base + (unrolled - lag)
        self.four = (unrolled - lag) % 4
        self.two = (unrolled - lag) % 2
        self.dma = base * 4 + 16 * ((unrolled - lag) // 4 + 1)
        self.active = not isinstance(base, int) or 0 <= self.n < count


def wait(eng, sem, value):
    if not isinstance(value, int) or value > 0:
        eng.wait_ge(sem, value)


def done(eng, sem, g):
    wait(eng, sem, g.n + 1)


def free(eng, sem, g, ring=2):
    wait(eng, sem, g.n + 1 - ring)


def gnn_kernel(nc, x, adj, W1, att_src1, att_dst1, b1, W2, att_src2, att_dst2, b2, Wq, Wk, Wv, Wo, out):
    G, N, D = x.shape
    H, F = att_src1.shape
    HF = H * F
    KD = D // 128
    NH, DK = 8, D // 8
    HALF = HF // 2 + 2 * (H // 2)
    SCALE = float(DK) ** -0.5

    ctx = ExitStack()
    with ctx:
        def sb(name, shape, dt=F32):
            return ctx.enter_context(nc.sbuf_tensor(name, shape, dt))

        def sem(name):
            return ctx.enter_context(nc.semaphore(name))

        ident = sb("ident", [128, 128])
        ident16 = sb("ident16", [128, 128], F16)
        pick = sb("pick", [2 * H, H, 128], F16)
        offdiag = sb("offdiag", [128, 128])
        ones = sb("ones", [128, 128])
        minus_half = sb("minus_half", [128, 1])
        pause = sb("pause", [128, 1])
        w1 = sb("w1", [128, KD, 2, HALF])
        w2 = sb("w2", [128, H, D + 2])
        proj = sb("proj", [128, KD, 4, D])
        w1_split = sb("w1_split", [128, 2, KD, 2, HALF], F16)
        proj_split = sb("proj_split", [128, 2, KD, 4, D], F16)
        largest = sb("largest", [128, 6])
        largest_all = sb("largest_all", [128, 6])
        power = sb("power", [128, 6])
        scale = sb("scale", [128, 6])
        q_power = sb("q_power", [128, 2])
        z_power = sb("z_power", [128, 2])
        absent = sb("absent", [128, 2, N])
        out_power = sb("out_power", [128, 1])
        b1_all = sb("b1_all", [128, HF])
        b2_all = sb("b2_all", [128, D])
        att1 = sb("att1", [128, 2, HF])
        att2 = sb("att2", [128, 2, D])
        prod = sb("prod", [128, 4, HF])
        prod2 = sb("prod2", [128, 4, HF])

        x_in = sb("x_in", [128, 4, D])
        adj_in = sb("adj_in", [128, 4, N], I32)
        mask_gat = sb("mask_gat", [128, 4, N], BF16)
        mask_mha = sb("mask_mha", [128, 4, N], BF16)
        stats = sb("stats", [128, 2, 2, 6])
        mv = sb("mv", [128, 2, 2, 2])
        var = sb("var", [128, 2, 2])
        rstd = sb("rstd", [128, 2, 2])
        z = sb("z", [128, 2, 2, D])
        hT = sb("hT", [128, 2, 2, D], F16)
        xl = sb("xl", [128, 2, HF])
        a_split = sb("a_split", [128, 2, 2, H], F16)
        aT = sb("aT", [2 * H, 2, N], F16)
        b = sb("b", [128, 2, H])
        rz = sb("rz", [128, 2, HF])
        lr = sb("lr", [128, 2, HF])
        nmx = sb("nmx", [128, 2, H])
        eT = sb("eT", [128, 2, HF])
        sm = sb("sm", [128, 2, H])
        rs = sb("rs", [128, 2, H])
        eTn = sb("eTn", [128, 2, HF])
        en = sb("en", [128, 2, HF])
        ex = sb("ex", [128, 2, HF])
        ex1 = sb("ex1", [128, 2, HF])
        h1T = sb("h1T", [128, 2, HF])
        xl2 = sb("xl2", [128, 2, D])
        ab2 = sb("ab2", [128, 2, 2])
        diag2 = sb("diag2", [128, 2, N])
        rz2 = sb("rz2", [128, 2, N])
        lr2 = sb("lr2", [128, 2, N])
        nmx2 = sb("nmx2", [128, 2, 1])
        eT2 = sb("eT2", [128, 2, N])
        sm2 = sb("sm2", [128, 2, 1])
        rs2 = sb("rs2", [128, 2, 1])
        en2 = sb("en2", [128, 2, N])
        x1 = sb("x1", [128, 4, D])
        h2T = sb("h2T", [128, 2, 2, D], F16)
        qkT = sb("qkT", [128, 2, 2, 4, N], F16)
        vv = sb("vv", [128, 2, 2, NH, DK + 1], F16)
        top3 = sb("top3", [128, 2, NH])
        nmx3 = sb("nmx3", [128, 2, NH])
        e3 = sb("e3", [128, 2, NH, N])
        e3T = sb("e3T", [128, 2, 2, NH, N], F16)
        rs3 = sb("rs3", [128, 2, NH])
        att = sb("att", [128, 2, D])
        attT = sb("attT", [128, 2, 2, D], F16)
        x_out = sb("x_out", [128, 4, D])

        bank = ctx.enter_context(nc.psum_tensor("bank", [128, 8, 512], F32))
        XL, EM, X2, AV, Z2, Z = bank[:, 0:2, :], bank[:, 2:4, :], bank[:, 4], bank[:, 5], bank[:, 6], bank[:, 7]
        QK, ET2, T3, V, O2, S = bank[:, 0], bank[:, 4], bank[:, 5], bank[:, 1], bank[:, 6], bank[:, 2:4, :]
        AT = bank[0:2 * H, 5, 0:N // 2].bitcast(F16)
        T2, ET, WO, T1, O1 = bank[:, 7], bank[:, 7], bank[:, 5], bank[:, 0], bank[:, 6]

        names = """ident_set ones_set pick_set w1_in w2_in proj_in w1_prod w1_set w2_prod w2_set largest_set largest_all_set power_set scale_set z_power_set q_power_set w_scaled
            w1_high w1_low split_high split_low
            absent_set masks_set att_scaled stats_set mv_set var_set rstd_set z_set
            stats2_set mv2_set var2_set rstd2_set z2_set
            t1_done hT_high hT_set xl_done xl_set b_set a_high a_set at_done aT_set zsc_done rz_set lr_set nmx_set eT_set rs_set eTn_set
            et_done en_set o1_done ex_set ex1_set h1T_set x2_done xl2_set ab2_set diag2_set zsc2_done rz2_set lr2_set
            nmx2_set eT2_set rs2_set et2_done en2_set o2_done x1_set t2_done h2T_high h2T_set qk_done qkT_high qkT_set v_done
            vv_high vv_set s_half s_done top3_set nmx3_set e3_set em_done e3T_high e3T_set av_done rs3_set att_set t3_done attT_high attT_set wo_done
            x_out_set""".split()
        s = {n: sem(n) for n in names}
        x_here = [sem(f"x_here{i}") for i in range(4)]
        adj_here = [sem(f"adj_here{i}") for i in range(4)]
        stored = [sem(f"stored{i}") for i in range(4)]

        def head_at(j):
            return j // 4 + (0, 4, 2, 6)[j % 4]

        def steps(eng, body, peeled=0, before=None):
            def step(base, unrolled):
                body({lag: Graph(base, unrolled, lag, G) for lag in (L_, P_, A_, B_, C_, D_)})

            for t in range(2 * UNROLL):
                if before and t in before:
                    before[t]()
                step(t - t % UNROLL, t % UNROLL)
            with eng.Fori(2 * UNROLL, G - peeled - UNROLL + 1, UNROLL) as t:
                for u in range(UNROLL):
                    step(t, u)
            for t in range(G - peeled, G + D_):
                step(t - t % UNROLL, t % UNROLL)

        def run(body_functions, graphs):
            for function, phase in body_functions:
                if graphs[phase].active:
                    function(graphs[phase])

        block = ctx.enter_context(nc.Block())

        @block.sync
        def _(sp):
            def load(g):
                free(sp, s["x1_set"], g, 4)
                sp.dma_start(x_in[:, g.four, :], x[bass.ds(g.n, 1)].rearrange("a n d -> (a n) d")).then_inc(x_here[g.four], 16)
                free(sp, s["masks_set"], g, 4)
                sp.dma_start(adj_in[:, g.four, :], adj[bass.ds(g.n, 1)].rearrange("a n d -> (a n) d")).then_inc(adj_here[g.four], 16)

            def store(g):
                done(sp, s["x_out_set"], g)
                sp.dma_start(out[bass.ds(g.n, 1)].rearrange("a n d -> (a n) d"), x_out[:, g.four, :]).then_inc(stored[g.four], 16)

            load(Graph(0, 0, 0, G))
            for k in range(KD):
                sp.dma_start(w1[:, k, :, 0:HF // 2], W1[k * 128:(k + 1) * 128, :].rearrange("p (a c) -> p a c", a=2)).then_inc(s["w1_in"], 16)
            for k in range(2):
                sp.dma_start(att1[:, k, :], (att_src1, att_dst1)[k].rearrange("h f -> (h f)").partition_broadcast(128)).then_inc(s["w1_in"], 16)
            sp.dma_start(b1_all[:, :], b1.partition_broadcast(128)).then_inc(s["w1_in"], 16)
            sp.dma_start(w2[:, :, 0:D], W2.rearrange("(k p) n -> p k n", p=128)).then_inc(s["w2_in"], 16)
            for k in range(2):
                sp.dma_start(att2[:, k, :], (att_src2, att_dst2)[k].rearrange("h f -> (h f)").partition_broadcast(128)).then_inc(s["w2_in"], 16)
            sp.dma_start(b2_all[:, :], b2.partition_broadcast(128)).then_inc(s["w2_in"], 16)
            for m, W in enumerate((Wq, Wk, Wv, Wo)):
                sp.dma_start(proj[:, :, m, :], W.rearrange("(k p) n -> p k n", p=128)).then_inc(s["proj_in"], 16)

            steps(sp, lambda graphs: run([(load, L_), (store, D_)], graphs), peeled=UNROLL)
            for n in range(4):
                sp.wait_ge(stored[n], 16 * (G // 4))

        @block.gpsimd
        def _(pool):
            pool.memset(ident[:, :], 0.0).then_inc(s["ident_set"], 1)
            pool.memset(offdiag[:, :], -BIG).then_inc(s["ident_set"], 1)
            pool.memset(ones[:, :], 1.0).then_inc(s["ones_set"], 1)
            pool.memset(minus_half[:, :], -0.5).then_inc(s["ones_set"], 1)
            pool.memset(vv[:, :, 0, :, DK:DK + 1], 1.0).then_inc(s["ones_set"], 1)
            pool.wait_ge(s["ident_set"], 2)
            for tile, fill in ((ident, 1.0), (offdiag, 0.0)):
                pool.affine_select(out=tile[:, :], in_=tile[:, :], compare_op=ALU.not_equal, fill=fill, base=0,
                                   pattern=[[-1, 128]], channel_multiplier=1).then_inc(s["ident_set"], 1)
            pool.wait_ge(s["ident_set"], 4)
            pool.tensor_copy(ident16[:, :], ident[:, :]).then_inc(s["ident_set"], 1)
            pool.memset(pick[:, :, :], 0.0).then_inc(s["pick_set"], 1)
            for n in range(2):
                pool.wait_ge(s["pick_set"], n + 1)
                pool.affine_select(out=pick[:, :, :], in_=pick[:, :, :], compare_op=ALU.not_equal, fill=1.0, base=-n * H,
                                   pattern=[[-1, H], [0, 128]], channel_multiplier=1).then_inc(s["pick_set"], 1)

            def products_w2():
                pool.wait_ge(s["largest_set"], 2)
                pool.partition_all_reduce(largest_all[:, 0:2], largest[:, 0:2], 128, bass.bass_isa.ReduceOp.max).then_inc(s["largest_all_set"], 1)
                pool.wait_ge(s["w2_in"], 16 * 4)
                pool.tensor_scalar(att2[:, 1, :], att2[:, 1, :], 1.0 - SLOPE, None, ALU.mult).then_inc(s["att_scaled"], 1)
                pool.wait_ge(s["att_scaled"], 2)
                for j in range(2):
                    for half in range(2):
                        pool.tensor_tensor(prod2[:, 2 * j + half, :].rearrange("p (a c) -> p a c", a=2), w2[:, 2 * half:2 * half + 2, 0:D],
                                           att2[:, j, :].unsqueeze(1).to_broadcast((128, 2, D)), ALU.mult).then_inc(s["w2_prod"], 1)
                pool.wait_ge(s["largest_set"], 3)
                pool.partition_all_reduce(largest_all[:, 2:6], largest[:, 2:6], 128, bass.bass_isa.ReduceOp.max).then_inc(s["largest_all_set"], 1)

            def split_low(m):
                pool.wait_ge(s["split_high"], m + 1)
                pool.wait_ge(s["w_scaled"], m + 1)
                pool.tensor_tensor(proj_split[:, 1, :, m, :], proj[:, :, m, :], proj_split[:, 0, :, m, :], ALU.subtract).then_inc(s["split_low"], 1)


            def diagonal2(g):
                done(pool, s["ab2_set"], g)
                free(pool, s["zsc2_done"], g)
                pool.tensor_tensor(diag2[:, g.two, :], ident[:, :], ab2[:, g.two, 0:1].to_broadcast((128, N)), ALU.mult).then_inc(s["diag2_set"], 1)

            def normalise(g):
                done(pool, s["rs_set"], g)
                done(pool, s["eT_set"], g)
                free(pool, s["et_done"], g)
                pool.tensor_tensor(eTn[:, g.two, :].rearrange("p (h n) -> p h n", h=H), eT[:, g.two, :].rearrange("p (h n) -> p h n", h=H),
                                   rs[:, g.two, :].unsqueeze(2).to_broadcast((128, H, N)), ALU.mult).then_inc(s["eTn_set"], 1)

            def rsqrt(g, which, var_set, free_sem, rstd_set):
                done(pool, s[var_set], g)
                free(pool, s[free_sem], g)
                pool.tensor_tensor(rstd[:, g.two, which:which + 1], var[:, g.two, which:which + 1], minus_half[:, :], ALU.pow).then_inc(s[rstd_set], 1)

            def rsqrt1(g):
                pool.wait_ge(adj_here[g.four], g.dma)
                free(pool, s["s_done"], g, 4)
                rsqrt(g, 0, "var_set", "z_set", "rstd_set")

            def masks(g):
                pool.tensor_scalar(absent[:, g.two, :], adj_in[:, g.four, :], 0.0, None, ALU.is_le).then_inc(s["absent_set"], 1)
                pool.tensor_scalar(mask_mha[:, g.four, :], adj_in[:, g.four, :], 0.0, -BIG, ALU.is_equal, ALU.mult)
                done(pool, s["absent_set"], g)
                pool.tensor_tensor(mask_gat[:, g.four, :], absent[:, g.two, :], offdiag[:, :], ALU.mult).then_inc(s["masks_set"], 1)

            def rsqrt2(g):
                rsqrt(g, 1, "var2_set", "z2_set", "rstd2_set")

            steps(pool, lambda graphs: run([
                (rsqrt1, P_), (masks, P_), (diagonal2, B_), (normalise, A_), (rsqrt2, B_),
            ], graphs), before={1: products_w2, 2: lambda: (split_low(0), split_low(1)), 3: lambda: split_low(2), 4: lambda: split_low(3)})

        @block.scalar
        def _(act):
            def split_high(m):
                act.wait_ge(s["scale_set"], 2)
                act.activation(proj_split[:, 0, :, m, :], proj[:, :, m, :], ACT.Copy, scale=scale[:, 2 + m:3 + m]).then_inc(s["split_high"], 1)
                act.activation(proj[:, :, m, :], proj[:, :, m, :], ACT.Copy, scale=scale[:, 2 + m:3 + m]).then_inc(s["w_scaled"], 1)

            def relu1(g):
                done(act, s["t1_done"], g)
                free(act, s["xl_done"], g)
                act.activation(hT[:, g.two, 0, :], T1[:, 0:D], ACT.Relu).then_inc(s["hT_high"], 1)

            def gat1_relu(g):
                done(act, s["zsc_done"], g)
                done(act, s["b_set"], g)
                free(act, s["lr_set"], g)
                for h in range(H):
                    ins = act.activation(rz[:, g.two, h * N:(h + 1) * N], Z[:, h * N:(h + 1) * N], ACT.Relu,
                                         bias=b[:, g.two, h:h + 1], scale=z_power[:, 1:2])
                ins.then_inc(s["rz_set"], 1)

            def gat2_relu(g):
                done(act, s["zsc2_done"], g)
                done(act, s["ab2_set"], g)
                free(act, s["lr2_set"], g)
                act.activation(rz2[:, g.two, :], Z2[:, 0:N], ACT.Relu, bias=ab2[:, g.two, 1:2], scale=1.0 - SLOPE).then_inc(s["rz2_set"], 1)

            def gat1_exp(g):
                done(act, s["nmx_set"], g)
                free(act, s["eTn_set"], g)
                for h in range(H):
                    ins = act.activation(eT[:, g.two, h * N:(h + 1) * N], lr[:, g.two, h * N:(h + 1) * N], ACT.Exp,
                                         bias=nmx[:, g.two, h:h + 1], accum_out=sm[:, g.two, h:h + 1])
                ins.then_inc(s["eT_set"], 1)

            def gat1_copy(g):
                done(act, s["et_done"], g)
                free(act, s["o1_done"], g)
                act.activation(en[:, g.two, :], ET[:, :], ACT.Copy).then_inc(s["en_set"], 1)

            def elu_exp(g):
                done(act, s["o1_done"], g)
                free(act, s["ex1_set"], g)
                act.activation(ex[:, g.two, :], O1[:, :], ACT.Exp).then_inc(s["ex_set"], 1)

            def aT_copy(g):
                done(act, s["at_done"], g)
                free(act, s["zsc_done"], g)
                act.activation(aT[:, g.two, :], AT, ACT.Copy).then_inc(s["aT_set"], 1)

            def elu_relu(g):
                done(act, s["ex_set"], g)
                free(act, s["h1T_set"], g)
                act.activation(ex1[:, g.two, :], ex[:, g.two, :], ACT.Relu, bias=1.0, scale=-1.0).then_inc(s["ex1_set"], 1)

            def gat2_exp(g):
                done(act, s["nmx2_set"], g)
                free(act, s["et2_done"], g)
                free(act, s["rs2_set"], g)
                act.activation(eT2[:, g.two, :], lr2[:, g.two, :], ACT.Exp, bias=nmx2[:, g.two, :],
                               accum_out=sm2[:, g.two, :]).then_inc(s["eT2_set"], 1)

            def gat2_copy(g):
                done(act, s["et2_done"], g)
                free(act, s["o2_done"], g)
                act.activation(en2[:, g.two, :], ET2[:, 0:N], ACT.Copy).then_inc(s["en2_set"], 1)

            def relu2(g):
                done(act, s["t2_done"], g)
                free(act, s["v_done"], g)
                act.activation(h2T[:, g.two, 0, :], T2[:, 0:D], ACT.Relu).then_inc(s["h2T_high"], 1)

            def qk_copy(g):
                done(act, s["qk_done"], g)
                free(act, s["s_done"], g)
                act.activation(qkT[:, g.two, 0, :, :], QK.rearrange("p (c n) -> p c n", c=4), ACT.Copy).then_inc(s["qkT_high"], 1)

            def v_copy(g):
                done(act, s["v_done"], g)
                free(act, s["av_done"], g)
                act.activation(vv[:, g.two, 0, :, 0:DK], V[:, 0:D].rearrange("p (h c) -> p h c", h=NH), ACT.Copy).then_inc(s["vv_high"], 1)

            def mha_exp(g, heads):
                for h in heads:
                    ins = act.activation(e3[:, g.two, h, :], S[:, h // 4, (h % 4) * N:(h % 4 + 1) * N], ACT.Exp,
                                         bias=nmx3[:, g.two, h:h + 1], scale=q_power[:, 1:2])
                return ins

            def mha_exp_first(g):
                done(act, s["nmx3_set"], g)
                free(act, s["em_done"], g)
                mha_exp(g, range(0, NH // 2))

            def mha_exp_last(g):
                mha_exp(g, range(NH // 2, NH)).then_inc(s["e3_set"], 1)

            def mha_copy(g):
                done(act, s["em_done"], g)
                free(act, s["av_done"], g)
                act.activation(e3T[:, g.two, 0, :, :], EM.rearrange("p b (h n) -> p (b h) n", h=4), ACT.Copy).then_inc(s["e3T_high"], 1)

            def att_copy(g):
                done(act, s["t3_done"], g)
                free(act, s["wo_done"], g)
                act.activation(attT[:, g.two, 0, :], T3[:, 0:D], ACT.Copy).then_inc(s["attT_high"], 1)

            steps(act, lambda graphs: run([
                (mha_exp_last, D_), (elu_exp, B_), (relu2, C_), (elu_relu, B_), (aT_copy, A_), (mha_copy, D_),
                (gat1_relu, A_), (qk_copy, C_), (gat1_exp, A_), (gat2_relu, B_), (v_copy, C_), (att_copy, D_),
                (gat2_exp, B_), (gat2_copy, B_), (gat1_copy, A_), (relu1, P_), (mha_exp_first, C_),
            ], graphs), before={
                1: lambda: act.wait_ge(s["z_power_set"], 2), 2: lambda: (split_high(0), split_high(1)),
                3: lambda: (split_high(2), act.wait_ge(s["q_power_set"], 3)), 4: lambda: split_high(3),
            })

        @block.vector
        def _(dve):
            high = slice(0, HF // 2)
            columns = slice(HF // 2, HALF)

            def power_of_two(first, last, count):
                dve.wait_ge(s["largest_all_set"], count)
                dve.tensor_scalar(power[:, first:last], largest_all[:, first:last], 2.0 ** -60, None, ALU.max).then_inc(s["power_set"], 1)
                dve.wait_ge(s["power_set"], 2 * count - 1)
                bits = power[:, first:last].bitcast(I32)
                dve.tensor_scalar(bits, bits, 0x7f800000, None, ALU.bitwise_and).then_inc(s["power_set"], 1)
                dve.wait_ge(s["power_set"], 2 * count)
                dve.tensor_scalar(scale[:, first:last].bitcast(I32), bits, -1.0, float(254 << 23), ALU.mult, ALU.add).then_inc(s["scale_set"], 1)

            def prepare_w1():
                dve.wait_ge(s["w1_in"], 16 * 5)
                dve.tensor_scalar(att1[:, 1, :], att1[:, 1, :], 1.0 - SLOPE, None, ALU.mult).then_inc(s["att_scaled"], 1)
                for j in range(2):
                    for k in range(KD):
                        if k == 0 and j == 1:
                            dve.wait_ge(s["att_scaled"], 1)
                        dve.tensor_tensor(prod[:, 2 * k + j, :].rearrange("p (a c) -> p a c", a=2), w1[:, k, :, high],
                                          att1[:, j, :].rearrange("p (a c) -> p a c", a=2), ALU.mult).then_inc(s["w1_prod"], 1)
                dve.tensor_reduce(largest[:, 0:1], w1[:, :, :, high], AX.XYZ, ALU.max, apply_absolute_value=True).then_inc(s["largest_set"], 1)
                dve.wait_ge(s["w1_prod"], 2 * KD)
                for k in range(KD):
                    for j in range(2):
                        dve.tensor_reduce(w1[:, k, :, HF // 2 + 2 * j:HF // 2 + 2 * j + 2],
                                          prod[:, 2 * k + j, :].rearrange("p (a h f) -> p a h f", a=2, h=2), AX.X, ALU.add).then_inc(s["w1_set"], 1)
                dve.wait_ge(s["w1_set"], 2 * KD)
                dve.tensor_reduce(largest[:, 1:2], w1[:, :, :, columns], AX.XYZ, ALU.max, apply_absolute_value=True).then_inc(s["largest_set"], 1)
                power_of_two(0, 2, 1)
                for n, slope in enumerate((SLOPE, 1.0 - SLOPE)):
                    dve.tensor_scalar(z_power[:, n:n + 1], power[:, 1:2], slope, None, ALU.mult).then_inc(s["z_power_set"], 1)
                dve.wait_ge(s["scale_set"], 1)
                parts = [(w1[:, :, :, part], w1_split[:, :, :, :, part], scale[:, i:i + 1]) for i, part in enumerate((high, columns))]
                for part, split, factor in parts:
                    dve.tensor_scalar(split[:, 0], part, factor, None, ALU.mult).then_inc(s["w1_high"], 1)
                dve.wait_ge(s["w1_high"], 2)
                for part, split, factor in parts:
                    for k in range(KD):
                        dve.scalar_tensor_tensor(out=split[:, 1, k], in0=part[:, k], scalar=factor, in1=split[:, 0, k],
                                                 op0=ALU.mult, op1=ALU.subtract).then_inc(s["w1_low"], 1)
                dve.wait_ge(s["z_power_set"], 2)
                dve.wait_ge(s["proj_in"], 16 * 4)
                dve.tensor_reduce(largest[:, 2:6], proj[:, :, :, :].rearrange("p k m n -> p m k n"), AX.XY, ALU.max,
                                  apply_absolute_value=True).then_inc(s["largest_set"], 1)

            def prepare_w2():
                power_of_two(2, 6, 2)
                dve.tensor_tensor(q_power[:, 0:1], power[:, 2:3], power[:, 3:4], ALU.mult).then_inc(s["q_power_set"], 1)
                dve.tensor_tensor(out_power[:, :], power[:, 4:5], power[:, 5:6], ALU.mult).then_inc(s["q_power_set"], 1)
                dve.wait_ge(s["q_power_set"], 2)
                dve.tensor_scalar(q_power[:, 1:2], q_power[:, 0:1], SCALE, None, ALU.mult).then_inc(s["q_power_set"], 1)
                dve.wait_ge(s["w2_prod"], 4)
                for j in range(2):
                    dve.tensor_reduce(w2[:, :, D + j:D + j + 1], prod2[:, 2 * j:2 * j + 2, :].rearrange("p b (a c) -> p b a c", a=2),
                                      AX.X, ALU.add).then_inc(s["w2_set"], 1)
                dve.wait_ge(s["q_power_set"], 3)

            def remainder(out_, in_, high_, sem_):
                dve.scalar_tensor_tensor(out=out_, in0=in_, scalar=0.0, in1=high_, op0=ALU.max, op1=ALU.subtract).then_inc(s[sem_], 1)

            def relu1_low(g):
                done(dve, s["hT_high"], g)
                free(dve, s["xl_done"], g)
                remainder(hT[:, g.two, 1, :], T1[:, 0:D], hT[:, g.two, 0, :], "hT_set")

            def relu2_low(g):
                done(dve, s["h2T_high"], g)
                free(dve, s["v_done"], g)
                remainder(h2T[:, g.two, 1, :], T2[:, 0:D], h2T[:, g.two, 0, :], "h2T_set")

            def mha_low(g):
                done(dve, s["e3T_high"], g)
                free(dve, s["av_done"], g)
                dve.tensor_tensor(e3T[:, g.two, 1, :, :], EM.rearrange("p b (h n) -> p (b h) n", h=4), e3T[:, g.two, 0, :, :],
                                  ALU.subtract).then_inc(s["e3T_set"], 1)

            def moments(g, which, src, stats_set, mv_set, var_set):
                dve.bn_stats(stats[:, g.two, which, :], src).then_inc(s[stats_set], 1)
                done(dve, s[stats_set], g)
                dve.memset(pause[:, :], 0.0)
                dve.bn_aggr(mv[:, g.two, which, :], stats[:, g.two, which, :]).then_inc(s[mv_set], 1)
                done(dve, s[mv_set], g)
                dve.tensor_scalar(var[:, g.two, which:which + 1], mv[:, g.two, which, 1:2], EPS, None, ALU.add).then_inc(s[var_set], 1)

            def normed(g, which, src, rstd_set, free_sem, z_set):
                done(dve, s[rstd_set], g)
                free(dve, s[free_sem], g)
                dve.tensor_scalar(z[:, g.two, which, :], src, mv[:, g.two, which, 0:1], rstd[:, g.two, which:which + 1],
                                  ALU.subtract, ALU.mult).then_inc(s[z_set], 1)

            def norm1_moments(g):
                dve.wait_ge(x_here[g.four], g.dma)
                moments(g, 0, x_in[:, g.four, :], "stats_set", "mv_set", "var_set")

            def norm1_apply(g):
                normed(g, 0, x_in[:, g.four, :], "rstd_set", "t1_done", "z_set")

            def elu(g):
                done(dve, s["ex1_set"], g)
                free(dve, s["x2_done"], g)
                dve.scalar_tensor_tensor(out=h1T[:, g.two, :], in0=ex1[:, g.two, :], scalar=-1.0, in1=O1[:, :],
                                         op0=ALU.mult, op1=ALU.max).then_inc(s["h1T_set"], 1)

            def xl_evac(g):
                done(dve, s["xl_done"], g)
                free(dve, s["at_done"], g)
                a, a_high, a_low = XL[:, :, HF // 2:HF // 2 + 2], *(a_split[:, g.two, n, :].rearrange("p (a h) -> p a h", a=2) for n in range(2))
                dve.tensor_copy(a_high, a).then_inc(s["a_high"], 1)
                free(dve, s["rz_set"], g)
                dve.tensor_scalar(b[:, g.two, :].rearrange("p (a h) -> p a h", a=2), XL[:, :, HF // 2 + 2:HALF], power[:, 1:2], None,
                                  ALU.mult).then_inc(s["b_set"], 1)
                done(dve, s["a_high"], g)
                dve.tensor_tensor(a_low, a, a_high, ALU.subtract).then_inc(s["a_set"], 1)
                free(dve, s["o1_done"], g)
                dve.scalar_tensor_tensor(out=xl[:, g.two, :].rearrange("p (a c) -> p a c", a=2), in0=XL[:, :, 0:HF // 2],
                                         scalar=power[:, 0:1], in1=b1_all[:, :].rearrange("p (a c) -> p a c", a=2),
                                         op0=ALU.mult, op1=ALU.add).then_inc(s["xl_set"], 1)

            def xl2_evac(g):
                done(dve, s["x2_done"], g)
                dve.tensor_copy(ab2[:, g.two, :], X2[:, D:D + 2]).then_inc(s["ab2_set"], 1)
                free(dve, s["o2_done"], g)
                dve.tensor_tensor(xl2[:, g.two, :], X2[:, 0:D], b2_all[:, :], ALU.add).then_inc(s["xl2_set"], 1)

            def att_norm(g):
                done(dve, s["av_done"], g)
                av = AV[:, 0:NH * (DK + 1)].rearrange("p (h c) -> p h c", h=NH)
                dve.reciprocal(rs3[:, g.two, :].unsqueeze(2), av[:, :, DK:DK + 1]).then_inc(s["rs3_set"], 1)
                done(dve, s["rs3_set"], g)
                free(dve, s["t3_done"], g)
                dve.scalar_tensor_tensor(out=att[:, g.two, :].rearrange("p (h c) -> p h c", h=NH), in0=av[:, :, 0:DK], scalar=0.0,
                                         in1=rs3[:, g.two, :].unsqueeze(2).to_broadcast((128, NH, DK)),
                                         op0=ALU.max, op1=ALU.mult).then_inc(s["att_set"], 1)

            def gat2_scores(g):
                done(dve, s["rz2_set"], g)
                free(dve, s["eT2_set"], g)
                dve.scalar_tensor_tensor(out=lr2[:, g.two, :], in0=Z2[:, 0:N], scalar=SLOPE, in1=rz2[:, g.two, :],
                                         op0=ALU.mult, op1=ALU.add).then_inc(s["lr2_set"], 1)
                done(dve, s["lr2_set"], g)
                dve.tensor_reduce(nmx2[:, g.two, :], lr2[:, g.two, :], AX.X, ALU.max, negate=True).then_inc(s["nmx2_set"], 1)

            def gat1_scores(g):
                done(dve, s["rz_set"], g)
                free(dve, s["eT_set"], g)
                dve.scalar_tensor_tensor(out=lr[:, g.two, :], in0=Z[:, :], scalar=z_power[:, 0:1], in1=rz[:, g.two, :],
                                         op0=ALU.mult, op1=ALU.add).then_inc(s["lr_set"], 1)
                done(dve, s["lr_set"], g)
                dve.tensor_reduce(nmx[:, g.two, :], lr[:, g.two, :].rearrange("p (h n) -> p h n", h=H), AX.X, ALU.max,
                                  negate=True).then_inc(s["nmx_set"], 1)

            def gat2_recip(g):
                done(dve, s["eT2_set"], g)
                dve.reciprocal(rs2[:, g.two, :], sm2[:, g.two, :]).then_inc(s["rs2_set"], 1)

            def qk_low(g):
                done(dve, s["qkT_high"], g)
                free(dve, s["s_done"], g)
                dve.tensor_tensor(qkT[:, g.two, 1, :, :], QK.rearrange("p (c n) -> p c n", c=4), qkT[:, g.two, 0, :, :],
                                  ALU.subtract).then_inc(s["qkT_set"], 1)

            def v_low(g):
                done(dve, s["vv_high"], g)
                free(dve, s["av_done"], g)
                dve.tensor_tensor(vv[:, g.two, 1, :, 0:DK], V[:, 0:D].rearrange("p (h c) -> p h c", h=NH), vv[:, g.two, 0, :, 0:DK],
                                  ALU.subtract).then_inc(s["vv_set"], 1)

            def residual1(g):
                done(dve, s["o2_done"], g)
                done(dve, s["rs2_set"], g)
                dve.scalar_tensor_tensor(out=x1[:, g.four, :], in0=O2[:, 0:D], scalar=rs2[:, g.two, :], in1=x_in[:, g.four, :],
                                         op0=ALU.mult, op1=ALU.add).then_inc(s["x1_set"], 1)

            def norm2_moments(g):
                done(dve, s["x1_set"], g)
                moments(g, 1, x1[:, g.four, :], "stats2_set", "mv2_set", "var2_set")

            def norm2_apply(g):
                normed(g, 1, x1[:, g.four, :], "rstd2_set", "t2_done", "z2_set")

            def gat1_recip(g):
                done(dve, s["eT_set"], g)
                dve.reciprocal(rs[:, g.two, :], sm[:, g.two, :]).then_inc(s["rs_set"], 1)

            def mha_max(g):
                done(dve, s["s_done"], g)
                dve.tensor_reduce(top3[:, g.two, :], S.rearrange("p b (h n) -> p (b h) n", h=4), AX.X, ALU.max,
                                  negate=True).then_inc(s["top3_set"], 1)
                done(dve, s["top3_set"], g)
                free(dve, s["e3_set"], g)
                dve.tensor_scalar(nmx3[:, g.two, :], top3[:, g.two, :], q_power[:, 1:2], None, ALU.mult).then_inc(s["nmx3_set"], 1)

            def att_low(g):
                done(dve, s["attT_high"], g)
                free(dve, s["wo_done"], g)
                dve.tensor_tensor(attT[:, g.two, 1, :], T3[:, 0:D], attT[:, g.two, 0, :], ALU.subtract).then_inc(s["attT_set"], 1)

            def residual2(g):
                done(dve, s["wo_done"], g)
                if not isinstance(g.n, int) or g.n >= 4:
                    dve.wait_ge(stored[g.four], g.dma - 16)
                dve.scalar_tensor_tensor(out=x_out[:, g.four, :], in0=WO[:, 0:D], scalar=out_power[:, 0:1], in1=x1[:, g.four, :],
                                         op0=ALU.mult, op1=ALU.add).then_inc(s["x_out_set"], 1)

            steps(dve, lambda graphs: run([
                (xl_evac, A_), (relu2_low, C_), (norm1_moments, P_), (elu, B_), (mha_low, D_), (gat1_scores, A_),
                (xl2_evac, B_), (qk_low, C_), (att_norm, D_), (norm1_apply, P_), (gat1_recip, A_), (gat2_scores, B_),
                (v_low, C_), (att_low, D_), (gat2_recip, B_), (mha_max, C_), (residual1, B_), (relu1_low, P_),
                (norm2_moments, B_), (norm2_apply, B_), (residual2, D_),
            ], graphs), before={1: prepare_w1, 2: prepare_w2})

        @block.tensor
        def _(pe):
            def w2_ready():
                pe.wait_ge(s["w2_set"], 2)
                pe.wait_ge(s["ones_set"], 3)

            first_waits = {
                0: lambda: pe.wait_ge(s["ident_set"], 5),
                1: lambda: (pe.wait_ge(s["w1_low"], 2 * KD), pe.wait_ge(s["pick_set"], 3)),
                2: w2_ready,
                3: lambda: pe.wait_ge(s["split_low"], 3),
                4: lambda: pe.wait_ge(s["split_low"], 4),
            }

            def chunks(tile):
                return tile.rearrange("p (k n) -> p k n", n=128)

            SPLIT = ((0, 0), (0, 1), (1, 0))

            def split_matmul(out_, groups):
                pairs = [p for group in groups for p in group]
                for n, (left, right) in enumerate(pairs):
                    ins = pe.matmul(out_, left, right, start=n == 0, stop=n == len(pairs) - 1)
                return ins

            def project1(g):
                done(pe, s["hT_set"], g)
                free(pe, s["vv_set"], g, 3)
                for a in range(2):
                    ins = split_matmul(XL[:, a, 0:HALF], [
                        [(chunks(hT[:, g.two, i, :])[:, k], w1_split[:, j, k, a, :]) for i, j in SPLIT] for k in range(KD)])
                ins.then_inc(s["xl_done"], 1)

            def mha_transpose(g):
                done(pe, s["e3_set"], g)
                for h in range(NH):
                    ins = pe.transpose(EM[:, h // 4, (h % 4) * N:(h % 4 + 1) * N], e3[:, g.two, h, :], ident[:, :])
                ins.then_inc(s["em_done"], 1)

            def project2(g):
                done(pe, s["h1T_set"], g)
                for k in range(H):
                    ins = pe.matmul(X2[:, 0:D + 2], h1T[:, g.two, k * F:(k + 1) * F], w2[:, k, :], start=k == 0, stop=k == H - 1)
                ins.then_inc(s["x2_done"], 1)

            def mha_av(g):
                done(pe, s["e3T_set"], g)
                done(pe, s["vv_set"], g)
                free(pe, s["x_out_set"], g, 1)
                wait(pe, s["aT_set"], min(g.n + 4, G) if isinstance(g.n, int) else g.n + 4)
                for j in range(NH):
                    h = head_at(j)
                    o = h * (DK + 1)
                    pe.matmul(AV[:, o:o + DK + 1], e3T[:, g.two, 0, j, :], vv[:, g.two, 0, h, :], start=True, stop=False)
                    pe.matmul(AV[:, o:o + DK], e3T[:, g.two, 0, j, :], vv[:, g.two, 1, h, 0:DK], start=False, stop=False)
                    ins = pe.matmul(AV[:, o:o + DK + 1], e3T[:, g.two, 1, j, :], vv[:, g.two, 0, h, :], start=False, stop=True)
                ins.then_inc(s["av_done"], 1)

            def scores2(g):
                done(pe, s["diag2_set"], g)
                done(pe, s["h1T_set"], g)
                pe.matmul(Z2[:, 0:N], ones[:, :], diag2[:, g.two, :], start=True, stop=False)
                pe.matmul(Z2[:, 0:N], mask_gat[:, g.four, :], ident16[:, :], start=False, stop=True).then_inc(s["zsc2_done"], 1)

            def transpose_a(g):
                done(pe, s["a_set"], g)
                wait(pe, s["x_out_set"], g.n - 3)
                pe.transpose(AT, a_split[:, g.two, :, :].rearrange("p s h -> p (s h)"), ident16[:, :]).then_inc(s["at_done"], 1)

            def scores1(g):
                done(pe, s["aT_set"], g)
                done(pe, s["masks_set"], g)
                free(pe, s["h2T_set"], g, 2)
                for h in range(H):
                    pe.matmul(Z[:, h * N:(h + 1) * N], mask_gat[:, g.four, :], ident16[:, :], start=True, stop=False)
                    ins = pe.matmul(Z[:, h * N:(h + 1) * N], pick[:, h, :], aT[:, g.two, :], start=False, stop=True)
                ins.then_inc(s["zsc_done"], 1)

            def qk(g):
                done(pe, s["h2T_set"], g)
                wait(pe, s["xl_set"], min(g.n + 3, G) if isinstance(g.n, int) else g.n + 3)
                for c in range(4):
                    ins = split_matmul(QK[:, c * N:(c + 1) * N], [
                        [(proj_split[:, i, k, c // 2, (c % 2) * 128:(c % 2 + 1) * 128], chunks(h2T[:, g.two, j, :])[:, k]) for i, j in SPLIT]
                        for k in range(KD)])
                ins.then_inc(s["qk_done"], 1)

            def transpose2(g):
                done(pe, s["eT2_set"], g)
                done(pe, s["xl2_set"], g)
                pe.transpose(ET2[:, 0:N], eT2[:, g.two, :], ident[:, :]).then_inc(s["et2_done"], 1)

            def att_transpose(g):
                done(pe, s["att_set"], g)
                for k in range(KD):
                    ins = pe.transpose(T3[:, k * N:(k + 1) * N], att[:, g.two, k * 128:(k + 1) * 128], ident[:, :])
                ins.then_inc(s["t3_done"], 1)

            def project_v(g):
                split_matmul(V[:, 0:D], [
                    [(chunks(h2T[:, g.two, i, :])[:, k], proj_split[:, j, k, 2, :]) for i, j in SPLIT] for k in range(KD)]).then_inc(s["v_done"], 1)

            def aggregate2(g):
                done(pe, s["en2_set"], g)
                pe.matmul(O2[:, 0:D], en2[:, g.two, :], xl2[:, g.two, :], start=True, stop=True).then_inc(s["o2_done"], 1)

            def scores3(g, columns):
                for col in columns:
                    for b in range(2):
                        pe.matmul(S[:, b, col * N:(col + 1) * N], ident16[:, :], mask_mha[:, g.four, :], start=True, stop=False)
                    for b in range(2):
                        h = head_at(4 * b + col)
                        r = slice(DK * (h % 4), DK * (h % 4 + 1))
                        for n, (i, j) in enumerate(SPLIT):
                            ins = pe.matmul(S[:, b, col * N:(col + 1) * N], qkT[r, g.two, i, h // 4, :], qkT[r, g.two, j, 2 + h // 4, :],
                                            start=False, stop=n == 2)
                return ins

            def scores3_first(g):
                done(pe, s["qkT_set"], g)
                wait(pe, s["e3T_set"], g.n)
                scores3(g, (0, 1)).then_inc(s["s_half"], 1)

            def scores3_last(g):
                done(pe, s["s_half"], g)
                scores3(g, (2, 3)).then_inc(s["s_done"], 1)

            def norm2_transpose(g):
                done(pe, s["z2_set"], g)
                for k in range(KD):
                    ins = pe.transpose(T2[:, k * N:(k + 1) * N], z[:, g.two, 1, k * 128:(k + 1) * 128], ident[:, :])
                ins.then_inc(s["t2_done"], 1)

            def transpose1(g):
                done(pe, s["eTn_set"], g)
                for h in range(H):
                    ins = pe.transpose(ET[:, h * N:(h + 1) * N], eTn[:, g.two, h * N:(h + 1) * N], ident[:, :])
                ins.then_inc(s["et_done"], 1)

            def project_out(g):
                done(pe, s["attT_set"], g)
                split_matmul(WO[:, 0:D], [
                    [(chunks(attT[:, g.two, i, :])[:, k], proj_split[:, j, k, 3, :]) for i, j in SPLIT] for k in range(KD)]).then_inc(s["wo_done"], 1)

            def norm1_transpose(g):
                done(pe, s["z_set"], g)
                wait(pe, s["qkT_set"], g.n - 2)
                for k in range(KD):
                    ins = pe.transpose(T1[:, k * N:(k + 1) * N], z[:, g.two, 0, k * 128:(k + 1) * 128], ident[:, :])
                ins.then_inc(s["t1_done"], 1)

            def aggregate1(g):
                done(pe, s["en_set"], g)
                done(pe, s["xl_set"], g)
                wait(pe, s["x1_set"], g.n)
                for h in range(H):
                    ins = pe.matmul(O1[:, h * N:(h + 1) * N], xl[:, g.two, h * F:(h + 1) * F], en[:, g.two, h * N:(h + 1) * N], start=True, stop=True)
                ins.then_inc(s["o1_done"], 1)

            steps(pe, lambda graphs: run([
                (project1, A_), (norm2_transpose, C_), (mha_transpose, D_), (transpose_a, A_), (scores1, A_), (qk, C_),
                (project2, B_), (mha_av, D_), (project_v, C_), (scores2, B_), (scores3_first, C_), (att_transpose, D_),
                (scores3_last, C_), (norm1_transpose, P_), (transpose2, B_), (transpose1, A_), (aggregate2, B_),
                (project_out, D_), (aggregate1, A_),
            ], graphs), before=first_waits)


_INS = ['x', 'adj', 'L0_gnn_W1', 'L0_gnn_att_src1', 'L0_gnn_att_dst1', 'L0_gnn_b1', 'L0_gnn_W2', 'L0_gnn_att_src2',
        'L0_gnn_att_dst2', 'L0_gnn_b2', 'L1_gnn_Wq', 'L1_gnn_Wk', 'L1_gnn_Wv', 'L1_gnn_Wo']


def kernel(**inputs):
    import numpy as _np
    import concourse.bacc as _bacc
    from concourse import mybir as _mybir
    from concourse.bass_utils import run_bass_kernel_spmd as _run

    nc = _bacc.Bacc("TRN2", target_bir_lowering=False, num_devices=1)
    arrays, args = {}, []
    for name in _INS:
        a = _np.ascontiguousarray(inputs[name])
        arrays[f"in_{name}_dram"] = a
        args.append(nc.dram_tensor(f"in_{name}_dram", a.shape, _mybir.dt.from_np(a.dtype), kind="ExternalInput").ap())
    shape = _np.shape(inputs["x"])
    args.append(nc.dram_tensor("out_dram", shape, _mybir.dt.float32, kind="ExternalOutput").ap())
    gnn_kernel(nc, *args)
    r = _run(nc, [arrays], core_ids=[0])
    return r.results[0]["out_dram"]
```
